# Optimizing a Trainium2 kernel written in Bass

```python
import numpy as np
import jax
import jax.numpy as jnp

def _softmax(x, axis=-1):
    return jax.nn.softmax(x, axis=axis)
def _gelu(x):
    return jax.nn.gelu(x, approximate=True)
def _silu(x):
    return jax.nn.silu(x)
def _sigmoid(x):
    return jax.nn.sigmoid(x)
def _layernorm(x, axis=-1, eps=1e-5):
    m = jnp.mean(x, axis=axis, keepdims=True)
    v = jnp.var(x, axis=axis, keepdims=True)
    return (x - m) / jnp.sqrt(v + eps)
def _scatter_add(tgt, idx, src, axis=0):
    return tgt.at[idx].add(src)
def _segment_sum(src, seg, n):
    return jax.ops.segment_sum(src, seg, n)

kernel_name = 'mk_adj_ffn_d1_adj_256_331435'

def setup_inputs(seed: int = 0):
    np.random.seed(seed)
    _w = jnp.asarray
    def _rec_inputs():
        import jax
        import jax.numpy as jnp
        _gk = jax.random.key(seed)
        x = -0.0001546 + 1 * jax.random.normal(jax.random.fold_in(_gk, 1), (128, 128, 256), jnp.float32)
        _a = jax.random.bernoulli(jax.random.fold_in(_gk, 2), 0.125, (128, 128))
        _a = jnp.logical_or(_a, jnp.swapaxes(_a, -1, -2))
        _a = jnp.logical_or(_a, jnp.eye(128, dtype=bool))
        _af = _a.astype(jnp.float32)
        _af = _af * jax.random.uniform(jax.random.fold_in(_gk, 3), (128, 128), jnp.float32, 0.05, 0.999927)
        adj = _af
        return x, adj
    x, adj = _rec_inputs()
    def _L0_gnn_setup():
        import jax, jax.numpy as jnp
        import numpy as np
        B, N, D = (4096, 128, 256)
        key = jax.random.key(seed)
        ks = jax.random.split(key, 6)
        return {'label': jax.random.normal(ks[0], (B, N, D), dtype=jnp.float32), 'adj_in': jax.random.uniform(ks[1], (N, N), dtype=jnp.float32), 'adj_out': jax.random.uniform(ks[2], (N, N), dtype=jnp.float32), 'edge_bias': jnp.zeros((N, D), dtype=jnp.float32), 'gate_weight': jax.random.normal(ks[3], (D, 1), dtype=jnp.float32) * (6.0 / (D + 1)) ** 0.5, 'bias_gate': jnp.zeros((N, 1), dtype=jnp.float32), 'out_edge_bias': jnp.zeros((N, D), dtype=jnp.float32), 'out_gate_weight': jax.random.normal(ks[4], (D, 1), dtype=jnp.float32) * (6.0 / (D + 1)) ** 0.5, 'out_bias_gate': jnp.zeros((N, 1), dtype=jnp.float32), 'loop_gate': jax.random.normal(ks[5], (D, 1), dtype=jnp.float32) * (6.0 / (D + 1)) ** 0.5}
    _L0_gnn_all = _L0_gnn_setup()
    _L0_gnn_in = {k: v for k, v in _L0_gnn_all.items() if k in ('edge_bias', 'gate_weight', 'bias_gate', 'out_edge_bias', 'out_gate_weight', 'out_bias_gate', 'loop_gate', )}
    del _L0_gnn_all

    def _L0_ffn_setup():
        import jax, jax.numpy as jnp
        import numpy as np
        BN_EPS = 0.001

        def _bn(h, g, b, m, v):
            return g * (h - m) * jax.lax.rsqrt(v + BN_EPS) + b
        key = jax.random.key(seed)
        ks = jax.random.split(key, 8)
        B, F, Df = (256, 64, 256)
        E, H, D = (8, 256, 256)
        s1 = 1.0 / np.sqrt(Df)
        s2 = 1.0 / np.sqrt(H)
        return {'x': jax.random.normal(ks[0], (B, F, Df), jnp.float32), 'Wr': jax.random.normal(ks[1], (Df, E), jnp.float32) * s1, 'br': jnp.zeros((E,), jnp.float32), 'W1': jax.random.normal(ks[2], (E, Df, H), jnp.float32) * s1, 'b1': jnp.zeros((E, H), jnp.float32), 'g1': jnp.ones((E, H), jnp.float32), 'be1': jnp.zeros((E, H), jnp.float32), 'm1': jnp.zeros((E, H), jnp.float32), 'v1': jnp.ones((E, H), jnp.float32), 'W2': jax.random.normal(ks[3], (E, H, H), jnp.float32) * s2, 'b2': jnp.zeros((E, H), jnp.float32), 'g2': jnp.ones((E, H), jnp.float32), 'be2': jnp.zeros((E, H), jnp.float32), 'm2': jnp.zeros((E, H), jnp.float32), 'v2': jnp.ones((E, H), jnp.float32), 'Wo': jax.random.normal(ks[4], (E, H, D), jnp.float32) * s2, 'bo': jnp.zeros((E, D), jnp.float32)}
    _L0_ffn_all = _L0_ffn_setup()
    _L0_ffn_in = {k: v for k, v in _L0_ffn_all.items() if k in ('Wr', 'br', 'W1', 'b1', 'g1', 'be1', 'm1', 'v1', 'W2', 'b2', 'g2', 'be2', 'm2', 'v2', 'Wo', 'bo', )}
    del _L0_ffn_all

    return {
        "x": x,
        "adj": adj,
        "L0_gnn_edge_bias": _L0_gnn_in["edge_bias"],
        "L0_gnn_gate_weight": _L0_gnn_in["gate_weight"],
        "L0_gnn_bias_gate": _L0_gnn_in["bias_gate"],
        "L0_gnn_out_edge_bias": _L0_gnn_in["out_edge_bias"],
        "L0_gnn_out_gate_weight": _L0_gnn_in["out_gate_weight"],
        "L0_gnn_out_bias_gate": _L0_gnn_in["out_bias_gate"],
        "L0_gnn_loop_gate": _L0_gnn_in["loop_gate"],
        "L0_ffn_Wr": _L0_ffn_in["Wr"],
        "L0_ffn_br": _L0_ffn_in["br"],
        "L0_ffn_W1": _L0_ffn_in["W1"],
        "L0_ffn_b1": _L0_ffn_in["b1"],
        "L0_ffn_g1": _L0_ffn_in["g1"],
        "L0_ffn_be1": _L0_ffn_in["be1"],
        "L0_ffn_m1": _L0_ffn_in["m1"],
        "L0_ffn_v1": _L0_ffn_in["v1"],
        "L0_ffn_W2": _L0_ffn_in["W2"],
        "L0_ffn_b2": _L0_ffn_in["b2"],
        "L0_ffn_g2": _L0_ffn_in["g2"],
        "L0_ffn_be2": _L0_ffn_in["be2"],
        "L0_ffn_m2": _L0_ffn_in["m2"],
        "L0_ffn_v2": _L0_ffn_in["v2"],
        "L0_ffn_Wo": _L0_ffn_in["Wo"],
        "L0_ffn_bo": _L0_ffn_in["bo"],
    }

def reference(x, adj, L0_gnn_edge_bias, L0_gnn_gate_weight, L0_gnn_bias_gate, L0_gnn_out_edge_bias, L0_gnn_out_gate_weight, L0_gnn_out_bias_gate, L0_gnn_loop_gate, L0_ffn_Wr, L0_ffn_br, L0_ffn_W1, L0_ffn_b1, L0_ffn_g1, L0_ffn_be1, L0_ffn_m1, L0_ffn_v1, L0_ffn_W2, L0_ffn_b2, L0_ffn_g2, L0_ffn_be2, L0_ffn_m2, L0_ffn_v2, L0_ffn_Wo, L0_ffn_bo):
    import jax
    import jax.numpy as jnp
    def _L0_gnn_ref(label, adj_in, adj_out, edge_bias, gate_weight, bias_gate, out_edge_bias, out_gate_weight, out_bias_gate, loop_gate):
        import jax, jax.numpy as jnp
        import numpy as np
        B, N, D = (4096, 128, 256)
        h = label
        origin = jax.lax.stop_gradient(jnp.where(adj_in <= 0, adj_in, 1.0))
        h_in = jnp.einsum('mn,bnd->bmd', origin * adj_in, h)
        in_gate = jnp.einsum('bnd,do->bno', h, gate_weight) + bias_gate
        msg_in = (h_in + edge_bias) * jax.nn.sigmoid(in_gate)
        h_out = jnp.einsum('mn,bnd->bmd', origin.T * adj_out, h)
        out_gate = jnp.einsum('bnd,do->bno', h, out_gate_weight) + out_bias_gate
        msg_out = (h_out + out_edge_bias) * jax.nn.sigmoid(out_gate)
        lp_gate = jnp.einsum('bnd,do->bno', h, loop_gate)
        msg_loop = h * jax.nn.sigmoid(lp_gate)
        return jax.nn.relu(msg_in + msg_out + msg_loop)

    def _L0_ffn_ref(x, Wr, br, W1, b1, g1, be1, m1, v1, W2, b2, g2, be2, m2, v2, Wo, bo):
        import jax, jax.numpy as jnp
        import numpy as np
        BN_EPS = 0.001

        def _bn(h, g, b, m, v):
            return g * (h - m) * jax.lax.rsqrt(v + BN_EPS) + b
        feat = jnp.mean(x, axis=0)
        w = jax.nn.softmax(feat @ Wr + br, axis=-1)
        h = jnp.einsum('bfd,edh->bfeh', x, W1) + b1
        h = jax.nn.relu(_bn(h, g1, be1, m1, v1))
        h = jnp.einsum('bfeh,ehk->bfek', h, W2) + b2
        h = jax.nn.relu(_bn(h, g2, be2, m2, v2))
        y = jnp.einsum('bfeh,ehd->bfed', h, Wo) + bo
        return jnp.einsum('bfed,fe->bfd', y, w)

    x = x + _L0_gnn_ref(_layernorm(x, axis=-1), adj, adj, L0_gnn_edge_bias, L0_gnn_gate_weight, L0_gnn_bias_gate, L0_gnn_out_edge_bias, L0_gnn_out_gate_weight, L0_gnn_out_bias_gate, L0_gnn_loop_gate)
    x = x + _L0_ffn_ref(_layernorm(x, axis=-1), L0_ffn_Wr, L0_ffn_br, L0_ffn_W1, L0_ffn_b1, L0_ffn_g1, L0_ffn_be1, L0_ffn_m1, L0_ffn_v1, L0_ffn_W2, L0_ffn_b2, L0_ffn_g2, L0_ffn_be2, L0_ffn_m2, L0_ffn_v2, L0_ffn_Wo, L0_ffn_bo)
    return x


_drawn_inputs = setup_inputs


def setup_inputs(seed=0):
    import zlib

    import numpy as np

    out = dict(_drawn_inputs(seed))
    spreads = {'L0_gnn_edge_bias': (0.0, 0.576),
     'L0_gnn_bias_gate': (0.0, 0.61),
     'L0_gnn_out_edge_bias': (0.0, 0.57),
     'L0_gnn_out_bias_gate': (0.0, 0.64),
     'L0_ffn_br': (0.0, 0.774),
     'L0_ffn_b1': (0.0, 0.8),
     'L0_ffn_g1': (1.0, 0.6),
     'L0_ffn_be1': (0.0, 0.8),
     'L0_ffn_m1': (0.0, 0.8),
     'L0_ffn_v1': (1.0, 0.6),
     'L0_ffn_b2': (0.0, 0.8),
     'L0_ffn_g2': (1.0, 0.6),
     'L0_ffn_be2': (0.0, 0.8),
     'L0_ffn_m2': (0.0, 0.8),
     'L0_ffn_v2': (1.0, 0.6),
     'L0_ffn_bo': (0.0, 0.689)}
    factors = {'L0_ffn_Wr': 8.0}
    for name, (base, spread) in spreads.items():
        noise = np.random.default_rng([zlib.crc32(name.encode()), seed]).standard_normal(out[name].shape)
        drawn = base * np.exp(spread * noise) if base else spread * noise
        out[name] = jnp.asarray(drawn.astype(out[name].dtype))
    for name, factor in factors.items():
        out[name] = (out[name] * factor).astype(out[name].dtype)
    return out
```

```python
from contextlib import ExitStack

import concourse.bass as bass
from concourse import mybir

ALU = mybir.AluOpType
ACT = mybir.ActivationFunctionType
AX_X = mybir.AxisListType.X
F32 = mybir.dt.float32
F32R = mybir.dt.float32r

P = 128
LN_EPS = 1e-5
BN_EPS = 1e-3


def adj_ffn_kernel(
    nc: bass.Bass,
    x: bass.AP,
    adj: bass.AP,
    edge_bias: bass.AP,
    gate_weight: bass.AP,
    bias_gate: bass.AP,
    out_edge_bias: bass.AP,
    out_gate_weight: bass.AP,
    out_bias_gate: bass.AP,
    loop_gate: bass.AP,
    Wr: bass.AP,
    br: bass.AP,
    W1: bass.AP,
    b1: bass.AP,
    g1: bass.AP,
    be1: bass.AP,
    m1: bass.AP,
    v1: bass.AP,
    W2: bass.AP,
    b2: bass.AP,
    g2: bass.AP,
    be2: bass.AP,
    m2: bass.AP,
    v2: bass.AP,
    Wo: bass.AP,
    bo: bass.AP,
    out: bass.AP,
):
    B, N, D = x.shape
    E = W1.shape[0]
    Q = 4
    NQ = B // Q
    KC = D // P
    R = Q * N
    QD = Q * D
    RING = 4
    NG = 3
    NL = 3
    N_CONST = 20
    assert N == P and D == W1.shape[2] == 2 * P and R == 512 and NQ % RING == 0
    assert NQ // RING == E, "phase A splits one expert's weights in each turn of its loop"

    x1_dram = nc.dram_tensor("x1_scratch", [NQ, N, QD], F32, kind="Internal").ap()

    with ExitStack() as ctx:
        def sb(name, shape, dt=F32):
            return ctx.enter_context(nc.sbuf_tensor(name, shape, dt))

        def sem(name):
            return ctx.enter_context(nc.semaphore(name))

        WCOLS = KC * D
        HW = KC * R
        EC = E * KC

        GR = NG * KC + NG

        ident = sb("ident", [P, P])
        ones = sb("ones", [P, P])
        neg_half = sb("neg_half", [P, 2 * EC])
        neg_one = sb("neg_one", [P, Q])
        w_hi = sb("w_hi", [P, NL, E * WCOLS], F32R)
        w_lo = sb("w_lo", [P, NL, E * WCOLS], F32R)
        rstd2 = sb("rstd2", [P, B])
        shift2 = sb("shift2", [P, B])
        bn_scale = sb("bn_scale", [P, 2, EC])
        bn_shift = sb("bn_shift", [P, 2, EC])
        acc = sb("acc", [P, QD])
        wr_sb = sb("wr_sb", [P, KC, E])
        br_sb = sb("br_sb", [1, E])
        bo_sb = sb("bo_sb", [E, D])
        feat_half = sb("feat_half", [P, 2 * D])
        feat = sb("feat", [P, D])
        featT = sb("featT", [P, D])
        neg_max = sb("neg_max", [P, 1])
        expo = sb("expo", [P, E])
        expo_sum = sb("expo_sum", [P, 1])
        expo_inv = sb("expo_inv", [P, 1])
        w_soft = sb("w_soft", [P, E])
        w_bcast = sb("w_bcast", [P, E, N])
        wT = sb("wT", [E, N])
        bo_mix = sb("bo_mix", [P, D])

        with ExitStack() as side_a:
            def sba(name, shape, dt=F32):
                return side_a.enter_context(nc.sbuf_tensor(name, shape, dt))

            x_ring = sba("x_ring", [P, RING, Q, D])
            h_ring = sba("h_ring", [P, RING, Q, D])
            x1_buf = sba("x1_buf", [P, 2, Q, D])
            x2_buf = sba("x2_buf", [P, 2, Q, D])
            t_buf = sba("t_buf", [P, 2, Q, D])
            hT = sba("hT", [P, KC, Q, N])
            w_raw = sba("w_raw", [P, NL, WCOLS])
            ident_r = sba("ident_r", [P, P], F32R)
            in_matT = sba("in_matT", [P, P])
            out_matT = sba("out_matT", [P, P])
            edge_hi = sba("edge_hi", [P, 2, D], F32R)
            edge_lo = sba("edge_lo", [P, 2, D], F32R)
            gate_cols = sba("gate_cols", [P, GR])
            bn6 = sba("bn6", [P, 2, Q, 6])
            mv1 = sba("mv1", [P, RING, Q, 2])
            mv2 = sba("mv2", [P, RING, Q, 2])
            var_eps = sba("var_eps", [P, 2, Q])
            neg_mu = sba("neg_mu", [P, 2, Q])
            rstd1 = sba("rstd1", [P, RING, Q])
            shift1 = sba("shift1", [P, RING, Q])
            gates = sba("gates", [P, 2, Q, NG])
            adj_sb = sba("adj_sb", [P, P])
            adj_min = sba("adj_min", [P, P])
            origin = sba("origin", [P, P])
            in_mat = sba("in_mat", [P, P])
            gate_rows = sba("gate_rows", [GR, P])
            edge_raw = sba("edge_raw", [P, 2, D])
            bn_rows = sba("bn_rows", [EC, 2, 5, P])
            bn_cols = sba("bn_cols", [P, 2, 5, EC])
            bn_var = sba("bn_var", [P, 2, EC])
            bn_rstd = sba("bn_rstd", [P, 2, EC])
            bn_diff = sba("bn_diff", [P, 2, EC])
            bn_prod = sba("bn_prod", [P, 2, EC])

        z1 = sb("z1", [P, HW])
        z2 = sb("z2", [P, HW])
        x1_in = sb("x1_in", [P, 2, Q, D])
        x2_in = sb("x2_in", [P, Q, D])
        yT = sb("yT", [P, KC, Q, N])
        out_buf = sb("out_buf", [P, 2, Q, D])
        w_diag = sb("w_diag", [P, E, N])
        xh = sb("xh", [P, 2, HW], F32R)
        xl = sb("xl", [P, 2, HW], F32R)
        h1h = sb("h1h", [P, 2, HW], F32R)
        h1l = sb("h1l", [P, 2, HW], F32R)
        h2h = sb("h2h", [P, HW], F32R)
        h2l = sb("h2l", [P, HW], F32R)

        bank = ctx.enter_context(nc.psum_tensor("bank", [P, 8, 512], F32))
        flat = bank[:, :, :].rearrange("p k c -> p (k c)")
        hT_ps = flat[:, 0:HW].rearrange("p (c q n) -> p c q n", c=KC, q=Q)
        gate_ps = bank[:, 6, 0:Q * NG].rearrange("p (q g) -> p q g", g=NG)
        xT_ps = flat[:, 6 * 512:8 * 512].rearrange("p (c q n) -> p c q n", c=KC, q=Q)
        y_ps = flat[:, 6 * 512:8 * 512].rearrange("p (q d) -> p q d", q=Q)

        s_const = sem("constants_loaded")
        s_adj_in = sem("adj_loaded")
        s_ident0 = sem("ident_zeroed")
        s_ident = sem("ident_ready")
        s_fill = sem("fills_ready")
        s_setup = sem("setup_dve_step")
        s_adjT = sem("adj_transposed")
        s_inT = sem("in_mat_transposed")
        s_mats = sem("matrices_ready")
        s_bnT = sem("bn_transposed")
        s_bnvar = sem("bn_variance_ready")
        s_bnrstd = sem("bn_rstd_ready")
        s_bn = sem("bn_dve_step")
        s_x = [sem(f"x_loaded{i}") for i in range(RING)]
        s_w = [sem(f"w_loaded{i}") for i in range(NL)]
        s_whi = sem("w_hi_ready")
        s_wlo = sem("w_lo_ready")
        s_bn6 = [sem("x_stats"), sem("x1_stats")]
        s_mv = [sem("x_mean_var"), sem("x1_mean_var")]
        s_step = [sem("rsqrt1_step"), sem("rsqrt2_step")]
        s_rs = [sem("rstd1_ready"), sem("rstd2_ready")]
        s_h = sem("h_ready")
        s_hT_ps = sem("h_transposed")
        s_hT = sem("hT_ready")
        s_gate_ps = sem("gate_logits")
        s_gate = sem("gates_ready")
        s_msg = sem("messages_ready")
        s_t1 = sem("in_message_gated")
        s_t2 = sem("out_message_added")
        s_t3 = sem("loop_message_added")
        s_x1 = sem("x1_ready")
        s_x1st = [sem(f"x1_stored{i}") for i in range(2)]
        s_x2 = sem("x2_ready")
        s_acc = sem("x2_summed")
        s_soft = sem("softmax_dve_step")
        s_featT = sem("feat_transposed")
        s_logit = sem("logits_ready")
        s_expo = sem("expo_ready")
        s_wT = sem("w_transposed")
        s_mix = sem("bo_mix_psum_ready")
        s_bc = sem("w_broadcast_psum_ready")
        s_wb = sem("w_broadcast_ready")
        s_xb = [sem(f"x1_loaded{i}") for i in range(2)]
        s_x2b = sem("x2_normed")
        s_xT = sem("x2_transposed")
        s_xh = sem("x2T_hi_ready")
        s_xl = sem("x2T_lo_ready")
        s_res = sem("residual_ready")
        s_l1 = sem("layer1_psum")
        s_z1 = sem("layer1_relu")
        s_h1h = sem("h1_hi_ready")
        s_h1l = sem("h1_lo_ready")
        s_l2 = sem("layer2_psum")
        s_z2 = sem("layer2_relu")
        s_z2w = sem("layer2_weighted")
        s_h2h = sem("h2_hi_ready")
        s_h2l = sem("h2_lo_ready")
        s_l3 = sem("layer3_summed")
        s_yT = sem("yT_ready")
        s_y = sem("y_transposed")
        s_out = sem("out_ready")
        s_outst = sem("out_stored")

        block = ctx.enter_context(nc.Block())

        def exists(k, j):
            return not isinstance(k, int) or 0 <= RING * k + j < NQ

        def turns(eng, turn, after_first=lambda: None):
            for j in range(-3, RING):
                turn(0, j)
            after_first()
            with eng.Fori(1, NQ // RING - 1) as k:
                for j in range(RING):
                    turn(k, j)
            for j in range(RING + 2):
                turn(NQ // RING - 1, j)

        def tiles(eng, tile):
            tile(0, 0, 0)
            with eng.Fori(0, (NQ - 2) // 2) as k:
                tile(k * 2 + 1, k, 1)
                tile(k * 2 + 2, k + 1, 0)
            tile(NQ - 1, NQ // 2 - 1, 1)

        def is_first(t):
            return isinstance(t, int) and t == 0

        def is_last(t):
            return isinstance(t, int) and t == NQ - 1

        def before(t, e, lag):
            if e >= lag:
                return t, e - lag
            return None if is_first(t) else (t - 1, e - lag + E)

        def unit(t, e):
            return t * E + e

        def w_at(t, layer, e, c, h):
            o = (e * KC + c) * D + h * P
            return t[:, layer, o:o + P]

        w_dram = [w.rearrange("e (c p) h -> p e c h", p=P) for w in (W1, W2, Wo)]

        @block.sync
        def _(sp):
            def load_x(k, j):
                sp.dma_start(x_ring[:, j % RING],
                             x[bass.ds((k * RING + j) * Q, Q), :, :].rearrange("b n d -> n b d"),
                             ).then_inc(s_x[j % RING], 16)

            sp.dma_start(adj_sb[:], adj).then_inc(s_adj_in, 16)
            for j in range(RING):
                load_x(0, j)

            def turn(k, j):
                if not exists(k, j):
                    return
                sp.wait_ge(s_x1, k * RING + j + 1)
                sp.dma_start(x1_dram[bass.ds(k * RING + j, 1), :, :].rearrange("a n c -> n (a c)"),
                             x1_buf[:, j % 2].rearrange("p q d -> p (q d)")).then_inc(s_x1st[j % 2], 16)
                if exists(k, j + RING):
                    load_x(k, j + RING)
                if 0 <= j < NL:
                    if not (isinstance(k, int) and k == 0):
                        sp.wait_ge(s_wlo, (k - 1) * NL + j + 1)
                    sp.dma_start(w_raw[:, j, :].rearrange("p (a c h) -> p a c h", a=1, c=KC),
                                 w_dram[j][:, bass.ds(k, 1), :, :]).then_inc(s_w[j], 16)

            turns(sp, turn)

            def load_x1(t, par):
                sp.dma_start(x1_in[:, par].rearrange("p q d -> p (q d)"),
                             x1_dram[bass.ds(t, 1), :, :].rearrange("a n c -> n (a c)")
                             ).then_inc(s_xb[par], 16)

            for i in range(2):
                sp.wait_ge(s_x1st[i], 16 * (NQ // 2))
            sp.wait_ge(s_acc, NQ + 1)
            sp.wait_ge(s_bn, 3)
            sp.wait_ge(s_wlo, NL * E)
            load_x1(0, 0)
            load_x1(1, 1)

            def store(t, par):
                sp.wait_ge(s_out, t + 1)
                sp.dma_start(out[bass.ds(t * Q, Q), :, :].rearrange("b n d -> n b d"),
                             x1_in[:, par]).then_inc(s_outst, 16)

            def tile(t, half, par):
                if not is_first(t):
                    store(t - 1, 1 - par)
                    if not is_last(t):
                        sp.wait_ge(s_outst, t * 16)
                        load_x1(t + 1, 1 - par)

            tiles(sp, tile)
            store(NQ - 1, 1)
            sp.wait_ge(s_outst, 16 * NQ)

        @block.gpsimd
        def _(pool):
            nc.gpsimd.memset(ident[:], 0.0).then_inc(s_ident0, 1)
            nc.gpsimd.memset(ones[:], 1.0).then_inc(s_fill, 1)
            nc.gpsimd.memset(neg_half[:], -0.5).then_inc(s_fill, 1)
            nc.gpsimd.memset(neg_one[:], -1.0).then_inc(s_fill, 1)
            nc.gpsimd.memset(gate_rows[:], 0.0).then_inc(s_fill, 1)
            pool.wait_ge(s_ident0, 1)
            nc.gpsimd.affine_select(out=ident[:], in_=ident[:], compare_op=ALU.not_equal, fill=1.0, base=0,
                                    pattern=[[-1, P]], channel_multiplier=1).then_inc(s_ident, 1)
            nc.gpsimd.memset(acc[:], 0.0).then_inc(s_acc, 1)
            pool.wait_ge(s_fill, 4)

            def rsqrt(which, i, mv, rstd, shift):
                nc.gpsimd.tensor_tensor(neg_mu[:, which], mv[:, :, 0], neg_one[:],
                                        ALU.mult).then_inc(s_step[which], 1)
                nc.gpsimd.tensor_scalar(var_eps[:, which], mv[:, :, 1], LN_EPS, None,
                                        ALU.add).then_inc(s_step[which], 1)
                pool.wait_ge(s_step[which], i * 3 + 2)
                nc.gpsimd.tensor_tensor(rstd, var_eps[:, which], neg_half[:, 0:Q],
                                        ALU.pow).then_inc(s_step[which], 1)
                pool.wait_ge(s_step[which], i * 3 + 3)
                nc.gpsimd.tensor_tensor(shift, neg_mu[:, which], rstd, ALU.mult).then_inc(s_rs[which], 1)

            def turn(k, j):
                s = k * RING + j
                if exists(k, j + 2):
                    slot = (j + 2) % RING
                    pool.wait_ge(s_mv[0], s + 3)
                    if exists(k, j + 1):
                        pool.wait_ge(s_rs[0], s + 2)
                    if exists(k, j - 2):
                        pool.wait_ge(s_h, s - 1)
                    rsqrt(0, s + 2, mv1[:, slot], rstd1[:, slot], shift1[:, slot])
                if exists(k, j - 1):
                    pool.wait_ge(s_mv[1], s)
                    if exists(k, j - 2):
                        pool.wait_ge(s_rs[1], s - 1)
                    cols = bass.ds((s - 1) * Q, Q)
                    rsqrt(1, s - 1, mv2[:, (j - 1) % RING], rstd2[:, cols], shift2[:, cols])
                if exists(k, j - 2):
                    pool.wait_ge(s_x2, s - 1)
                    pool.wait_ge(s_acc, s - 1)
                    nc.gpsimd.tensor_tensor(acc[:], acc[:], x2_buf[:, j % 2].rearrange("p q d -> p (q d)"),
                                            ALU.add).then_inc(s_acc, 1)
                if exists(k, j) and 1 <= j <= NL:
                    pool.wait_ge(s_whi, k * NL + j)
                    cols = bass.ds(k * WCOLS, WCOLS)
                    nc.gpsimd.tensor_tensor(w_lo[:, j - 1, cols], w_raw[:, j - 1, :],
                                            w_hi[:, j - 1, cols].bitcast(F32), ALU.subtract).then_inc(s_wlo, 1)

            def bn_rsqrt():
                pool.wait_ge(s_bnvar, 1)
                nc.gpsimd.tensor_tensor(bn_rstd[:].rearrange("p l c -> p (l c)"),
                                        bn_var[:].rearrange("p l c -> p (l c)"), neg_half[:],
                                        ALU.pow).then_inc(s_bnrstd, 1)

            turns(pool, turn, bn_rsqrt)

            def residual(t, par):
                pool.wait_ge(s_x2b, t + 1)
                nc.gpsimd.tensor_tensor(x1_in[:, par], x1_in[:, par],
                                        bo_mix[:, None, :].to_broadcast([P, Q, D]), ALU.add).then_inc(s_res, 1)

            pool.wait_ge(s_wb, 1)
            residual(0, 0)

            def tile(t, half, par):
                if not is_last(t):
                    residual(t + 1, 1 - par)

            tiles(pool, tile)

        @block.scalar
        def _(act):
            small = [
                (gate_rows[0:KC, :], gate_weight.rearrange("(c p) o -> c (p o)", p=P)),
                (gate_rows[KC:2 * KC, :], out_gate_weight.rearrange("(c p) o -> c (p o)", p=P)),
                (gate_rows[2 * KC:3 * KC, :], loop_gate.rearrange("(c p) o -> c (p o)", p=P)),
                (gate_rows[NG * KC:NG * KC + 1, :], bias_gate.rearrange("p o -> o p")),
                (gate_rows[NG * KC + 1:NG * KC + 2, :], out_bias_gate.rearrange("p o -> o p")),
                (edge_raw[:, 0, :], edge_bias),
                (edge_raw[:, 1, :], out_edge_bias),
            ] + [
                (bn_rows[:, layer, i, :], a.rearrange("e (c p) -> (e c) p", p=P))
                for layer, arrays in enumerate(((g1, be1, m1, v1, b1), (g2, be2, m2, v2, b2)))
                for i, a in enumerate(arrays)
            ] + [
                (wr_sb[:], Wr.rearrange("(c p) e -> p c e", p=P)),
                (br_sb[:], br.rearrange("(a e) -> a e", a=1)),
                (bo_sb[:], bo),
            ]
            assert len(small) == N_CONST
            act.wait_ge(s_fill, 4)
            for dst, src in small:
                act.dma_start(dst, src).then_inc(s_const, 16)

            def gate_in(s, j, p):
                act.wait_ge(s_msg, s * 2 + p + 1)
                for q in (2 * p, 2 * p + 1):
                    ins = nc.scalar.activation(t_buf[:, j % 2, q, :], bank[:, 2 + p, (q % 2) * D:(q % 2 + 1) * D],
                                               ACT.Copy, scale=gates[:, j % 2, q, 0:1])
                ins.then_inc(s_t1, 1)

            def turn(k, j):
                s = k * RING + j
                if exists(k, j):
                    act.wait_ge(s_gate, s + 1)
                    if exists(k, j - 2):
                        act.wait_ge(s_x1, s - 1)
                    gate_in(s, j, 0)
                if exists(k, j + 1):
                    act.wait_ge(s_hT_ps, s + 2)
                    if exists(k, j):
                        act.wait_ge(s_gate_ps, s + 1)
                    nc.scalar.activation(hT[:].rearrange("p c q n -> p (c q n)"), flat[:, 0:HW],
                                         ACT.Copy).then_inc(s_hT, 1)
                if exists(k, j):
                    gate_in(s, j, 1)
                if exists(k, j + 2):
                    slot = (j + 2) % RING
                    act.wait_ge(s_rs[0], s + 3)
                    if exists(k, j - 2):
                        act.wait_ge(s_x1, s - 1)
                    for q in range(Q):
                        ins = nc.scalar.activation(h_ring[:, slot, q, :], x_ring[:, slot, q, :], ACT.Identity,
                                                   bias=shift1[:, slot, q:q + 1], scale=rstd1[:, slot, q:q + 1])
                    ins.then_inc(s_h, 1)
                if exists(k, j + 1):
                    act.wait_ge(s_gate_ps, s + 2)
                    if exists(k, j - 1):
                        act.wait_ge(s_x1, s)
                    nc.scalar.activation(gates[:, (j + 1) % 2], gate_ps,
                                         ACT.Sigmoid).then_inc(s_gate, 1)
                if exists(k, j - 1):
                    act.wait_ge(s_rs[1], s)
                    if exists(k, j - 3):
                        act.wait_ge(s_acc, s - 1)
                    for q in range(Q):
                        col = bass.ds((s - 1) * Q + q, 1)
                        ins = nc.scalar.activation(x2_buf[:, (j - 1) % 2, q, :], x1_buf[:, (j - 1) % 2, q, :],
                                                   ACT.Identity, bias=shift2[:, col], scale=rstd2[:, col])
                    ins.then_inc(s_x2, 1)
                if exists(k, j) and 1 <= j <= NL:
                    act.wait_ge(s_w[j - 1], k * 16 + 16)
                    nc.scalar.activation(w_hi[:, j - 1, bass.ds(k * WCOLS, WCOLS)], w_raw[:, j - 1, :],
                                         ACT.Copy).then_inc(s_whi, 1)

            turns(act, turn)

            act.wait_ge(s_soft, 4)
            nc.scalar.activation(expo[:], bank[:, 4, 0:E], ACT.Exp, bias=neg_max[:],
                                 accum_out=expo_sum[:]).then_inc(s_expo, 1)

            def norm(t, half, par):
                act.wait_ge(s_xb[par], half * 16 + 16)
                if not is_first(t):
                    act.wait_ge(s_xT, t)
                for q in range(Q):
                    col = bass.ds(t * Q + q, 1)
                    ins = nc.scalar.activation(x2_in[:, q, :], x1_in[:, par, q, :], ACT.Identity,
                                               bias=shift2[:, col], scale=rstd2[:, col])
                ins.then_inc(s_x2b, 1)

            def x_hi(t, par):
                act.wait_ge(s_xT, t + 1)
                nc.scalar.activation(xh[:, par], xT_ps.rearrange("p c q n -> p (c q n)"),
                                     ACT.Copy).then_inc(s_xh, 1)

            def relu(layer, t, e):
                ready, z, used, done = ((s_l1, z1, s_h1l, s_z1), (s_l2, z2, s_h2l, s_z2))[layer]
                for c in range(KC):
                    act.wait_ge(ready, unit(t, e) * KC + c + 1)
                    if c == 0 and not (is_first(t) and e == 0):
                        act.wait_ge(used, unit(t, e))
                    i = e * KC + c
                    nc.scalar.activation(z[:, c * R:(c + 1) * R], bank[:, 2 * layer + c, :], ACT.Relu,
                                         bias=bn_shift[:, layer, i:i + 1],
                                         scale=bn_scale[:, layer, i:i + 1]).then_inc(done, 1)

            def yT_copy(t):
                act.wait_ge(s_l3, unit(t, E))
                nc.scalar.activation(yT[:].rearrange("p c q n -> p (c q n)"), flat[:, 4 * 512:6 * 512],
                                     ACT.Copy).then_inc(s_yT, 1)

            norm(0, 0, 0)
            x_hi(0, 0)

            def tile(t, half, par):
                for e in range(E):
                    if e == 2 and not is_first(t):
                        yT_copy(t - 1)
                    if e == 5 and not is_last(t):
                        norm(t + 1, half + par, 1 - par)
                    if e == 6 and not is_last(t):
                        act.wait_ge(s_l1, unit(t, 0) * KC) if not is_first(t) else None
                        x_hi(t + 1, 1 - par)
                    relu(0, t, e)
                    if before(t, e, 1):
                        relu(1, *before(t, e, 1))

            tiles(act, tile)
            relu(1, NQ - 1, E - 1)
            yT_copy(NQ - 1)

        @block.vector
        def _(dve):
            dve.wait_ge(s_adj_in, 16)
            nc.vector.tensor_scalar(adj_min[:], adj_sb[:], 0.0, None, ALU.min).then_inc(s_setup, 1)
            dve.wait_ge(s_setup, 1)
            nc.vector.scalar_tensor_tensor(origin[:], adj_sb[:], 0.0, adj_min[:], ALU.is_gt,
                                           ALU.add).then_inc(s_setup, 1)
            dve.wait_ge(s_setup, 2)
            nc.vector.tensor_tensor(in_mat[:], origin[:], adj_sb[:], ALU.mult).then_inc(s_setup, 1)
            dve.wait_ge(s_adjT, 1)
            nc.vector.tensor_tensor(out_matT[:], bank[:, 7, 0:P], origin[:], ALU.mult).then_inc(s_mats, 1)
            dve.wait_ge(s_inT, 1)
            nc.vector.tensor_copy(in_matT[:], bank[:, 5, 0:P]).then_inc(s_mats, 1)
            dve.wait_ge(s_ident, 1)
            nc.vector.tensor_copy(ident_r[:], ident[:]).then_inc(s_mats, 1)

            def stats(which, src, i):
                for q in range(Q):
                    ins = nc.vector.bn_stats(bn6[:, which, q, :], src[:, q, :])
                ins.then_inc(s_bn6[which], 1)

            def mean_var(which, dst):
                for q in range(Q):
                    ins = nc.vector.bn_aggr(dst[:, q, :], bn6[:, which, q, :])
                ins.then_inc(s_mv[which], 1)

            def turn(k, j):
                s = k * RING + j
                here, ahead = exists(k, j), exists(k, j + 3)
                slot = (j + 3) % RING
                if exists(k, j - 1):
                    dve.wait_ge(s_bn6[1], s)
                    if exists(k, j - RING):
                        dve.wait_ge(s_rs[1], s - RING + 1)
                if here:
                    for p in range(2):
                        dve.wait_ge(s_t1, s * 2 + p + 1)
                        for q in (2 * p, 2 * p + 1):
                            t = t_buf[:, j % 2, q, :]
                            ins = nc.vector.scalar_tensor_tensor(
                                t, bank[:, 4 + p, (q % 2) * D:(q % 2 + 1) * D], gates[:, j % 2, q, 1:2], t,
                                ALU.mult, ALU.add)
                        ins.then_inc(s_t2, 1)
                if exists(k, j - 1):
                    mean_var(1, mv2[:, (j - 1) % RING])
                if here:
                    for p in range(2):
                        dve.wait_ge(s_t2, s * 2 + p + 1)
                        for q in (2 * p, 2 * p + 1):
                            t = t_buf[:, j % 2, q, :]
                            ins = nc.vector.scalar_tensor_tensor(t, h_ring[:, j % RING, q, :],
                                                                 gates[:, j % 2, q, 2:3], t, ALU.mult, ALU.add)
                    ins.then_inc(s_t3, 1)
                if ahead:
                    dve.wait_ge(s_x[slot], (k + (j + 3) // RING) * 16 + 16)
                    if exists(k, j + 2):
                        dve.wait_ge(s_mv[0], s + 3)
                    stats(0, x_ring[:, slot], s + 3)
                if ahead:
                    dve.wait_ge(s_bn6[0], s + 4)
                    if exists(k, j - 1):
                        dve.wait_ge(s_rs[0], s)
                if here:
                    dve.wait_ge(s_t3, s + 1)
                    if exists(k, j - 2):
                        dve.wait_ge(s_x1st[j % 2], (k * 2 + j // 2) * 16)
                        dve.wait_ge(s_x2, s - 1)
                    nc.vector.scalar_tensor_tensor(
                        x1_buf[:, j % 2].rearrange("p q d -> p (q d)"),
                        t_buf[:, j % 2].rearrange("p q d -> p (q d)"), 0.0,
                        x_ring[:, j % RING].rearrange("p q d -> p (q d)"), ALU.max, ALU.add).then_inc(s_x1, 1)
                if ahead:
                    mean_var(0, mv1[:, slot])
                if here:
                    dve.wait_ge(s_x1, s + 1)
                    if exists(k, j - 1):
                        dve.wait_ge(s_mv[1], s)
                    stats(1, x1_buf[:, j % 2], s)

            dve.wait_ge(s_const, 16 * N_CONST)
            nc.vector.tensor_copy(edge_hi[:], edge_raw[:]).then_inc(s_mats, 1)
            dve.wait_ge(s_mats, 4)
            nc.vector.tensor_tensor(edge_lo[:], edge_raw[:], edge_hi[:].bitcast(F32),
                                    ALU.subtract).then_inc(s_mats, 1)
            G_, BE, M_, V_, B_ = range(5)
            dve.wait_ge(s_bnT, 1)
            nc.vector.tensor_copy(bn_cols[:].rearrange("p l i c -> p (l i c)"),
                                  bank[:, 7, 0:10 * EC]).then_inc(s_setup, 1)
            nc.vector.tensor_copy(gate_cols[:], bank[:, 7, 10 * EC:10 * EC + GR]).then_inc(s_mats, 1)
            dve.wait_ge(s_setup, 4)
            nc.vector.tensor_scalar(bn_var[:], bn_cols[:, :, V_, :], BN_EPS, None, ALU.add).then_inc(s_bnvar, 1)
            nc.vector.tensor_tensor(bn_diff[:], bn_cols[:, :, B_, :], bn_cols[:, :, M_, :],
                                    ALU.subtract).then_inc(s_bn, 1)

            turns(dve, turn)

            dve.wait_ge(s_bnrstd, 1)
            nc.vector.tensor_tensor(bn_scale[:], bn_cols[:, :, G_, :], bn_rstd[:], ALU.mult).then_inc(s_bn, 1)
            dve.wait_ge(s_bn, 2)
            nc.vector.tensor_tensor(bn_prod[:], bn_diff[:], bn_scale[:], ALU.mult).then_inc(s_bn, 1)
            dve.wait_ge(s_bn, 3)
            nc.vector.tensor_tensor(bn_shift[:], bn_prod[:], bn_cols[:, :, BE, :], ALU.add).then_inc(s_bn, 1)

            dve.wait_ge(s_acc, NQ + 1)
            nc.vector.tensor_tensor(feat_half[:], acc[:, 0:2 * D], acc[:, 2 * D:4 * D], ALU.add).then_inc(s_soft, 1)
            dve.wait_ge(s_soft, 1)
            nc.vector.tensor_tensor(feat[:], feat_half[:, 0:D], feat_half[:, D:2 * D], ALU.add).then_inc(s_soft, 1)
            dve.wait_ge(s_featT, 1)
            nc.vector.tensor_scalar(featT[:], bank[:, 5, 0:D], 1.0 / B, None, ALU.mult).then_inc(s_soft, 1)
            dve.wait_ge(s_logit, 1)
            nc.vector.tensor_reduce(neg_max[:], bank[:, 4, 0:E], AX_X, ALU.max, negate=True).then_inc(s_soft, 1)
            dve.wait_ge(s_expo, 1)
            nc.vector.reciprocal(expo_inv[:], expo_sum[:]).then_inc(s_soft, 1)
            dve.wait_ge(s_soft, 5)
            nc.vector.tensor_scalar(w_soft[:], expo[:], expo_inv[:], None, ALU.mult).then_inc(s_soft, 1)
            dve.wait_ge(s_soft, 6)
            dve.wait_ge(s_x1st[0], 16 * (NQ // 2))
            dve.wait_ge(s_x1st[1], 16 * (NQ // 2))
            dve.wait_ge(s_wlo, NL * E)
            for e in range(E):
                ins = nc.vector.tensor_scalar(w_diag[:, e, :], ident[:], w_soft[:, e:e + 1], None, ALU.mult)
            ins.then_inc(s_soft, 1)
            dve.wait_ge(s_wT, 1)
            nc.vector.tensor_copy(wT[:], bank[0:E, 5, 2 * P:3 * P]).then_inc(s_soft, 1)
            dve.wait_ge(s_mix, 1)
            nc.vector.tensor_copy(bo_mix[:], bank[:, 4, 0:D]).then_inc(s_wb, 1)
            dve.wait_ge(s_bc, 1)
            nc.vector.tensor_copy(w_bcast[:].rearrange("p e n -> p (e n)"),
                                  flat[:, 4 * 512:6 * 512]).then_inc(s_wb, 1)

            def x_lo(t, par):
                dve.wait_ge(s_xh, t + 1)
                nc.vector.tensor_tensor(xl[:, par], xT_ps.rearrange("p c q n -> p (c q n)"),
                                        xh[:, par].bitcast(F32), ALU.subtract).then_inc(s_xl, 1)

            def split1(t, e):
                i = unit(t, e)
                dve.wait_ge(s_z1, i * KC + KC)
                if before(t, e, 2):
                    dve.wait_ge(s_l2, (i - 1) * KC)
                nc.vector.tensor_copy(h1h[:, e % 2], z1[:]).then_inc(s_h1h, 1)
                dve.wait_ge(s_h1h, i + 1)
                nc.vector.tensor_tensor(h1l[:, e % 2], z1[:], h1h[:, e % 2].bitcast(F32),
                                        ALU.subtract).then_inc(s_h1l, 1)

            def split2(t, e):
                i = unit(t, e)
                dve.wait_ge(s_z2, i * KC + KC)
                z = z2[:].rearrange("p (a n) -> p a n", n=N)
                nc.vector.tensor_tensor(z, z, w_bcast[:, e:e + 1, :].to_broadcast([P, KC * Q, N]),
                                        ALU.mult).then_inc(s_z2w, 1)
                dve.wait_ge(s_z2w, i + 1)
                if before(t, e, 1):
                    dve.wait_ge(s_l3, i)
                nc.vector.tensor_copy(h2h[:], z2[:]).then_inc(s_h2h, 1)
                dve.wait_ge(s_h2h, i + 1)
                nc.vector.tensor_tensor(h2l[:], z2[:], h2h[:].bitcast(F32), ALU.subtract).then_inc(s_h2l, 1)

            def output(t, par):
                dve.wait_ge(s_y, t + 1)
                dve.wait_ge(s_res, t + 1)
                nc.vector.tensor_tensor(x1_in[:, par], y_ps, x1_in[:, par], ALU.add).then_inc(s_out, 1)

            x_lo(0, 0)

            def tile(t, half, par):
                for e in range(E):
                    if e == 3 and not is_first(t):
                        output(t - 1, 1 - par)
                    if e == 6 and not is_last(t):
                        x_lo(t + 1, 1 - par)
                    split1(t, e)
                    if before(t, e, 1):
                        if is_first(t) and e == 1:
                            dve.wait_ge(s_wb, 2)
                        split2(*before(t, e, 1))

            tiles(dve, tile)
            split2(NQ - 1, E - 1)
            output(NQ - 1, 1)

        @block.tensor
        def _(pe):
            pe.wait_ge(s_adj_in, 16)
            pe.wait_ge(s_ident, 1)
            nc.tensor.transpose(bank[:, 7, 0:P], adj_sb[:], ident[:]).then_inc(s_adjT, 1)
            pe.wait_ge(s_setup, 3)
            nc.tensor.transpose(bank[:, 5, 0:P], in_mat[:], ident[:]).then_inc(s_inT, 1)
            pe.wait_ge(s_const, 16 * N_CONST)
            pe.wait_ge(s_mats, 2)
            for layer in range(2):
                for i in range(5):
                    o = (layer * 5 + i) * EC
                    nc.tensor.transpose(bank[:, 7, o:o + EC], bn_rows[:, layer, i, :], ident[0:EC, 0:EC])
            nc.tensor.transpose(bank[:, 7, 10 * EC:10 * EC + GR], gate_rows[:], ident[0:GR, 0:GR]).then_inc(s_bnT, 1)

            def messages(s, k, j, p):
                if p == 0:
                    pe.wait_ge(s_h, s + 1)
                if exists(k, j - 1):
                    pe.wait_ge(s_t1, s * 2 + p - 1)
                    pe.wait_ge(s_t2, s * 2 + p - 1)
                moving = h_ring[:, j % RING, 2 * p:2 * p + 2, :]
                for i, matT in enumerate((in_matT, out_matT)):
                    dst = bank[:, 2 + 2 * i + p, :].rearrange("p (q d) -> p q d", q=2)
                    nc.tensor.matmul(dst, matT[:], moving, start=True, stop=False)
                    nc.tensor.matmul(dst, ident_r[:], edge_hi[:, i:i + 1, :].to_broadcast([P, 2, D]),
                                     start=False, stop=False)
                    ins = nc.tensor.matmul(dst, ident_r[:], edge_lo[:, i:i + 1, :].to_broadcast([P, 2, D]),
                                           start=False, stop=True)
                ins.then_inc(s_msg, 1)

            def turn(k, j):
                s = k * RING + j
                if exists(k, j):
                    messages(s, k, j, 0)
                if exists(k, j + 1):
                    pe.wait_ge(s_h, s + 2)
                    if exists(k, j):
                        pe.wait_ge(s_hT, s + 1)
                    for q in range(Q):
                        for c in range(KC):
                            ins = nc.tensor.transpose(hT_ps[:, c, q, :],
                                                      h_ring[:, (j + 1) % RING, q, c * P:(c + 1) * P], ident[:])
                    ins.then_inc(s_hT_ps, 1)
                if exists(k, j):
                    messages(s, k, j, 1)
                if exists(k, j + 1):
                    pe.wait_ge(s_hT, s + 2)
                    if isinstance(k, int) and s == -1:
                        pe.wait_ge(s_mats, 6)
                    if exists(k, j):
                        pe.wait_ge(s_gate, s + 1)
                    nc.tensor.matmul(gate_ps, ident[:], gate_cols[:, None, NG * KC:].to_broadcast([P, Q, NG]),
                                     start=True, stop=False, skip_group_check=True)
                    for q in range(Q):
                        for c in range(KC):
                            ins = nc.tensor.matmul(gate_ps[:, q, :], hT[:, c, q, :], gate_cols[:, c:NG * KC:KC],
                                                   start=False, stop=(q == Q - 1 and c == KC - 1),
                                                   skip_group_check=True)
                    ins.then_inc(s_gate_ps, 1)

            pe.wait_ge(s_fill, 4)
            turns(pe, turn)

            pe.wait_ge(s_soft, 2)
            for c in range(KC):
                ins = nc.tensor.transpose(bank[:, 5, c * P:(c + 1) * P], feat[:, c * P:(c + 1) * P], ident[:])
            ins.then_inc(s_featT, 1)
            pe.wait_ge(s_soft, 3)
            dst = bank[:, 4, 0:E]
            nc.tensor.matmul(dst, ones[0:1, :], br_sb[:], start=True, stop=False)
            for c in range(KC):
                ins = nc.tensor.matmul(dst, featT[:, c * P:(c + 1) * P], wr_sb[:, c, :], start=False,
                                       stop=(c == KC - 1))
            ins.then_inc(s_logit, 1)
            pe.wait_ge(s_soft, 6)
            nc.tensor.transpose(bank[0:E, 5, 2 * P:3 * P], w_soft[:], ident[:]).then_inc(s_wT, 1)
            pe.wait_ge(s_soft, 8)
            nc.tensor.matmul(bank[:, 4, 0:D], wT[:], bo_sb[:], start=True, stop=True).then_inc(s_mix, 1)
            pe.wait_ge(s_wb, 1)
            for i in range(2):
                ins = nc.tensor.matmul(bank[:, 4 + i, :], ones[:],
                                       w_diag[:, 4 * i:4 * i + 4, :].rearrange("p e n -> p (e n)"),
                                       start=True, stop=True)
            ins.then_inc(s_bc, 1)

            def x_transposes(t):
                pe.wait_ge(s_x2b, t + 1)
                for c in range(KC):
                    for q in range(Q):
                        ins = nc.tensor.transpose(xT_ps[:, c, q, :], x2_in[:, q, c * P:(c + 1) * P], ident[:])
                ins.then_inc(s_xT, 1)

            def y_transposes(t):
                pe.wait_ge(s_yT, t + 1)
                for q in range(Q):
                    for c in range(KC):
                        ins = nc.tensor.transpose(y_ps[:, q, c * P:(c + 1) * P], yT[:, c, q, :], ident[:])
                ins.then_inc(s_y, 1)

            def layer(n, e, h, dst, hi, lo, first=True, last=True):
                for c in range(KC):
                    rows = slice(c * R, (c + 1) * R)
                    whi, wlo = w_at(w_hi, n, e, c, h), w_at(w_lo, n, e, c, h)
                    nc.tensor.matmul(dst, whi, hi[:, rows], start=(first and c == 0), stop=False)
                    nc.tensor.matmul(dst, wlo, hi[:, rows], start=False, stop=False)
                    ins = nc.tensor.matmul(dst, whi, lo[:, rows], start=False, stop=(last and c == KC - 1))
                return ins

            def layer1(t, par, e):
                if e == 0:
                    pe.wait_ge(s_xh, t + 1)
                    pe.wait_ge(s_xl, t + 1)
                for h in range(KC):
                    if before(t, e, 1):
                        pe.wait_ge(s_z1, unit(t, e - 1) * KC + h + 1)
                    layer(0, e, h, bank[:, h, :], xh[:, par], xl[:, par]).then_inc(s_l1, 1)

            def layer2(t, e):
                i = unit(t, e)
                pe.wait_ge(s_h1h, i + 1)
                pe.wait_ge(s_h1l, i + 1)
                for h in range(KC):
                    if before(t, e, 1):
                        pe.wait_ge(s_z2, (i - 1) * KC + h + 1)
                    layer(1, e, h, bank[:, 2 + h, :], h1h[:, e % 2], h1l[:, e % 2]).then_inc(s_l2, 1)

            def layer3(t, e):
                pe.wait_ge(s_h2h, unit(t, e) + 1)
                pe.wait_ge(s_h2l, unit(t, e) + 1)
                if e == 0 and not is_first(t):
                    pe.wait_ge(s_yT, t)
                for h in range(KC):
                    ins = layer(2, e, h, bank[:, 4 + h, :], h2h, h2l, first=(e == 0), last=(e == E - 1))
                ins.then_inc(s_l3, 1)

            x_transposes(0)

            def tile(t, half, par):
                for e in range(E):
                    if e == 3 and not is_first(t):
                        y_transposes(t - 1)
                    if e == 6 and not is_last(t):
                        if not is_first(t):
                            pe.wait_ge(s_out, t)
                        else:
                            pe.wait_ge(s_xl, 1)
                        x_transposes(t + 1)
                    layer1(t, par, e)
                    if before(t, e, 1):
                        layer2(*before(t, e, 1))
                    if before(t, e, 2):
                        layer3(*before(t, e, 2))

            tiles(pe, tile)
            layer2(NQ - 1, E - 1)
            layer3(NQ - 1, E - 2)
            layer3(NQ - 1, E - 1)
            y_transposes(NQ - 1)


_INS = ['x', 'adj', 'L0_gnn_edge_bias', 'L0_gnn_gate_weight', 'L0_gnn_bias_gate', 'L0_gnn_out_edge_bias',
        'L0_gnn_out_gate_weight', 'L0_gnn_out_bias_gate', 'L0_gnn_loop_gate', 'L0_ffn_Wr', 'L0_ffn_br', 'L0_ffn_W1',
        'L0_ffn_b1', 'L0_ffn_g1', 'L0_ffn_be1', 'L0_ffn_m1', 'L0_ffn_v1', 'L0_ffn_W2', 'L0_ffn_b2', 'L0_ffn_g2',
        'L0_ffn_be2', 'L0_ffn_m2', 'L0_ffn_v2', 'L0_ffn_Wo', 'L0_ffn_bo']
_OUTS = [((128, 128, 256), 'float32')]


def kernel(**inputs):
    import numpy as _np
    import concourse.bacc as _bacc
    from concourse import mybir as _mybir
    from concourse.bass_utils import run_bass_kernel_spmd as _run

    nc = _bacc.Bacc("TRN2", target_bir_lowering=False, num_devices=1)
    arrays, args = {}, []
    for name in _INS:
        a = _np.ascontiguousarray(inputs[name])
        arrays[f"in_{name}_dram"] = a
        args.append(nc.dram_tensor(f"in_{name}_dram", a.shape, _mybir.dt.from_np(a.dtype), kind="ExternalInput").ap())
    for i, (shape, dtype) in enumerate(_OUTS):
        dt = _mybir.dt.from_np(_np.dtype(dtype))
        args.append(nc.dram_tensor(f"out_{i}_dram", shape, dt, kind="ExternalOutput").ap())
    adj_ffn_kernel(nc, *args)
    r = _run(nc, [arrays], core_ids=[0])
    got = tuple(r.results[0][f"out_{i}_dram"] for i in range(len(_OUTS)))
    return got[0]
```

```python
from contextlib import ExitStack

import concourse.bass as bass
from concourse import mybir

ALU = mybir.AluOpType
ACT = mybir.ActivationFunctionType
AX_X = mybir.AxisListType.X
F32 = mybir.dt.float32
F32R = mybir.dt.float32r

P = 128
LN_EPS = 1e-5
BN_EPS = 1e-3


def adj_ffn_kernel(
    nc: bass.Bass,
    x: bass.AP,
    adj: bass.AP,
    edge_bias: bass.AP,
    gate_weight: bass.AP,
    bias_gate: bass.AP,
    out_edge_bias: bass.AP,
    out_gate_weight: bass.AP,
    out_bias_gate: bass.AP,
    loop_gate: bass.AP,
    Wr: bass.AP,
    br: bass.AP,
    W1: bass.AP,
    b1: bass.AP,
    g1: bass.AP,
    be1: bass.AP,
    m1: bass.AP,
    v1: bass.AP,
    W2: bass.AP,
    b2: bass.AP,
    g2: bass.AP,
    be2: bass.AP,
    m2: bass.AP,
    v2: bass.AP,
    Wo: bass.AP,
    bo: bass.AP,
    out: bass.AP,
):
    B, N, D = x.shape
    E = W1.shape[0]
    Q = 4
    NQ = B // Q
    KC = D // P
    R = Q * N
    QD = Q * D
    RING = 4
    NG = 3
    NL = 3
    N_CONST, N_LATE = 7, 13
    N_WARM = 24
    assert N == P and D == W1.shape[2] == 2 * P and R == 512 and NQ % RING == 0
    assert NQ // RING == E, "phase A splits one expert's weights in each turn of its loop"

    x1_dram = nc.dram_tensor("x1_scratch", [NQ, N, QD], F32, kind="Internal").ap()

    with ExitStack() as ctx:
        def sb(name, shape, dt=F32):
            return ctx.enter_context(nc.sbuf_tensor(name, shape, dt))

        def sem(name):
            return ctx.enter_context(nc.semaphore(name))

        WCOLS = KC * D
        HW = KC * R
        EC = E * KC

        GR = NG * KC + NG

        ident = sb("ident", [P, P])
        ones = sb("ones", [P, P])
        neg_half = sb("neg_half", [P, 2 * EC])
        neg_one = sb("neg_one", [P, Q])
        w_hi = sb("w_hi", [P, NL, E * WCOLS], F32R)
        w_lo = sb("w_lo", [P, NL, E * WCOLS], F32R)
        rstd2 = sb("rstd2", [P, B])
        shift2 = sb("shift2", [P, B])
        bn_scale = sb("bn_scale", [P, 2, EC])
        bn_shift = sb("bn_shift", [P, 2, EC])
        acc = sb("acc", [P, QD])
        wr_sb = sb("wr_sb", [P, KC, E])
        br_sb = sb("br_sb", [1, E])
        bo_sb = sb("bo_sb", [E, D])
        featT = sb("featT", [P, D])
        neg_max = sb("neg_max", [P, 1])
        expo = sb("expo", [P, E])
        expo_sum = sb("expo_sum", [P, 1])
        expo_inv = sb("expo_inv", [P, 1])
        w_soft = sb("w_soft", [P, E])
        w_bcast = sb("w_bcast", [P, E, N])
        wT = sb("wT", [E, N])
        bo_mix = sb("bo_mix", [P, D])

        with ExitStack() as side_s:
            def sbs(name, shape, dt=F32):
                return side_s.enter_context(nc.sbuf_tensor(name, shape, dt))

            adj_sb = sbs("adj_sb", [P, P])
            adj_min = sbs("adj_min", [P, P])
            origin = sbs("origin", [P, P])
            in_mat = sbs("in_mat", [P, P])
            gate_rows = sbs("gate_rows", [GR, P])
            edge_raw = sbs("edge_raw", [P, 2, D])
            bn_rows = sbs("bn_rows", [EC, 2, 5, P])
            bn_cols = sbs("bn_cols", [P, 2, 5, EC])
            bn_var = sbs("bn_var", [P, 2, EC])
            bn_rstd = sbs("bn_rstd", [P, 2, EC])
            bn_diff = sbs("bn_diff", [P, 2, EC])
            bn_prod = sbs("bn_prod", [P, 2, EC])

        x1_even = sb("x1_even", [P, Q, D])
        x2_in = sb("x2_in", [P, Q, D])
        xh_even = sb("xh_even", [P, HW], F32R)
        xl_even = sb("xl_even", [P, HW], F32R)
        z1 = sb("z1", [P, HW])

        with ExitStack() as side_a:
            def sba(name, shape, dt=F32):
                return side_a.enter_context(nc.sbuf_tensor(name, shape, dt))

            x_ring = sba("x_ring", [P, RING, Q, D])
            h_ring = sba("h_ring", [P, RING, Q, D])
            hT = sba("hT", [P, KC, Q, N])
            in_matT = sba("in_matT", [P, P])
            out_matT = sba("out_matT", [P, P])
            ident_r = sba("ident_r", [P, P], F32R)
            edge_hi = sba("edge_hi", [P, 2, D], F32R)
            edge_lo = sba("edge_lo", [P, 2, D], F32R)
            t_buf = sba("t_buf", [P, 2, Q, D])
            x1_buf = sba("x1_buf", [P, 2, Q, D])
            x2_buf = sba("x2_buf", [P, 2, Q, D])
            w_raw = sba("w_raw", [P, NL, WCOLS])
            gate_cols = sba("gate_cols", [P, GR])
            bn6 = sba("bn6", [P, 2, Q, 6])
            mv1 = sba("mv1", [P, RING, Q, 2])
            mv2 = sba("mv2", [P, RING, Q, 2])
            var_eps = sba("var_eps", [P, 2, Q])
            neg_mu = sba("neg_mu", [P, 2, Q])
            rstd1 = sba("rstd1", [P, RING, Q])
            shift1 = sba("shift1", [P, RING, Q])
            gates = sba("gates", [P, 2, Q, NG])

        z2 = sb("z2", [P, HW])
        h1h = sb("h1h", [P, 2, HW], F32R)
        h1l = sb("h1l", [P, 2, HW], F32R)
        x1_odd = sb("x1_odd", [P, Q, D])
        xh_odd = sb("xh_odd", [P, HW], F32R)
        xl_odd = sb("xl_odd", [P, HW], F32R)
        w_diag = sb("w_diag", [P, E, N])
        yT = sb("yT", [P, KC, Q, N])
        h2h = sb("h2h", [P, HW], F32R)
        h2l = sb("h2l", [P, HW], F32R)
        x1_in, xh, xl = (x1_even, x1_odd), (xh_even, xh_odd), (xl_even, xl_odd)

        bank = ctx.enter_context(nc.psum_tensor("bank", [P, 8, 512], F32))
        flat = bank[:, :, :].rearrange("p k c -> p (k c)")
        hT_ps = flat[:, 0:HW].rearrange("p (c q n) -> p c q n", c=KC, q=Q)
        gate_ps = bank[:, 6, 0:Q * NG].rearrange("p (q g) -> p q g", g=NG)
        xT_ps = flat[:, 6 * 512:8 * 512].rearrange("p (c q n) -> p c q n", c=KC, q=Q)
        y_ps = flat[:, 6 * 512:8 * 512].rearrange("p (q d) -> p q d", q=Q)

        s_const = sem("constants_loaded")
        s_late = sem("late_constants_loaded")
        s_gateT = sem("gates_transposed")
        s_adj_in = sem("adj_loaded")
        s_ident0 = sem("ident_zeroed")
        s_ident = sem("ident_ready")
        s_fill = sem("fills_ready")
        s_setup = sem("setup_dve_step")
        s_adjT = sem("adj_transposed")
        s_inT = sem("in_mat_transposed")
        s_mats = sem("matrices_ready")
        s_bnT = sem("bn_transposed")
        s_bnvar = sem("bn_variance_ready")
        s_bnrstd = sem("bn_rstd_ready")
        s_bn = sem("bn_dve_step")
        s_x = [sem(f"x_loaded{i}") for i in range(RING)]
        s_w = [sem(f"w_loaded{i}") for i in range(NL)]
        s_whi = sem("w_hi_ready")
        s_wlo = sem("w_lo_ready")
        s_bn6 = [sem("x_stats"), sem("x1_stats")]
        s_mv = [sem("x_mean_var"), sem("x1_mean_var")]
        s_step = [sem("rsqrt1_step"), sem("rsqrt2_step")]
        s_rs = [sem("rstd1_ready"), sem("rstd2_ready")]
        s_h = sem("h_ready")
        s_hT_ps = sem("h_transposed")
        s_hT = sem("hT_ready")
        s_gate_ps = sem("gate_logits")
        s_gate = sem("gates_ready")
        s_msg = sem("messages_ready")
        s_t1 = sem("in_message_gated")
        s_t2 = sem("out_message_added")
        s_t3 = sem("loop_message_added")
        s_x1 = sem("x1_ready")
        s_x1st = [sem(f"x1_stored{i}") for i in range(2)]
        s_x2 = sem("x2_ready")
        s_x2last = sem("last_x2_ready")
        s_acc = sem("x2_summed")
        s_fold = sem("sum_folded")
        s_soft = sem("softmax_dve_step")
        s_featT = sem("feat_transposed")
        s_logit = sem("logits_ready")
        s_expo = sem("expo_ready")
        s_wT = sem("w_transposed")
        s_mix = sem("bo_mix_psum_ready")
        s_bc = sem("w_broadcast_psum_ready")
        s_wb = [sem(f"w_broadcast_ready{i}") for i in range(2)]
        s_bo = sem("bo_mix_ready")
        s_xb = [sem(f"x1_loaded{i}") for i in range(2)]
        s_x2b = sem("x2_normed")
        s_xT = sem("x2_transposed")
        s_xh = sem("x2T_hi_ready")
        s_xl = sem("x2T_lo_ready")
        s_res = sem("residual_ready")
        s_l1 = sem("layer1_psum")
        s_z1 = sem("layer1_relu")
        s_h1h = sem("h1_hi_ready")
        s_h1l = sem("h1_lo_ready")
        s_l2 = sem("layer2_psum")
        s_z2 = sem("layer2_relu")
        s_z2w = sem("layer2_weighted")
        s_h2h = sem("h2_hi_ready")
        s_h2l = sem("h2_lo_ready")
        s_l3 = sem("layer3_summed")
        s_yT = sem("yT_ready")
        s_y = sem("y_transposed")
        s_out = sem("out_ready")
        s_outst = sem("out_stored")

        block = ctx.enter_context(nc.Block())

        def exists(k, j):
            return not isinstance(k, int) or 0 <= RING * k + j < NQ

        def is_last_quad(k, j):
            return isinstance(k, int) and RING * k + j == NQ - 1

        def fill(turn, steps=range(-3, RING)):
            for j in steps:
                turn(0, j)

        def middle(eng, turn):
            with eng.Fori(1, NQ // RING - 1) as k:
                for j in range(RING):
                    turn(k, j)

        def drain(turn, steps=range(RING + 2)):
            for j in steps:
                turn(NQ // RING - 1, j)

        def tiles(eng, tile):
            tile(0, 0, 0)
            with eng.Fori(0, (NQ - 2) // 2) as k:
                tile(k * 2 + 1, k, 1)
                tile(k * 2 + 2, k + 1, 0)
            tile(NQ - 1, NQ // 2 - 1, 1)

        def is_first(t):
            return isinstance(t, int) and t == 0

        def is_last(t):
            return isinstance(t, int) and t == NQ - 1

        def before(t, e, lag):
            if e >= lag:
                return t, e - lag
            return None if is_first(t) else (t - 1, e - lag + E)

        def unit(t, e):
            return t * E + e

        def w_at(t, layer, e, c, h):
            o = (e * KC + c) * D + h * P
            return t[:, layer, o:o + P]

        w_dram = [w.rearrange("e (c p) h -> p e c h", p=P) for w in (W1, W2, Wo)]

        @block.sync
        def _(sp):
            def load_x(k, j):
                sp.dma_start(x_ring[:, j % RING],
                             x[bass.ds((k * RING + j) * Q, Q), :, :].rearrange("b n d -> n b d"),
                             ).then_inc(s_x[j % RING], 16)

            sp.dma_start(adj_sb[:], adj).then_inc(s_adj_in, 16)
            for j in range(RING):
                load_x(0, j)
            late = [
                (bn_rows[:, layer, i, :], a.rearrange("e (c p) -> (e c) p", p=P))
                for layer, arrays in enumerate(((g1, be1, m1, v1, b1), (g2, be2, m2, v2, b2)))
                for i, a in enumerate(arrays)
            ] + [
                (wr_sb[:], Wr.rearrange("(c p) e -> p c e", p=P)),
                (br_sb[:], br.rearrange("(a e) -> a e", a=1)),
                (bo_sb[:], bo),
            ]
            assert len(late) == N_LATE
            for dst, src in late:
                sp.dma_start(dst, src).then_inc(s_late, 16)

            def turn(k, j):
                if not exists(k, j):
                    return
                sp.wait_ge(s_x1, k * RING + j + 1)
                sp.dma_start(x1_dram[bass.ds(k * RING + j, 1), :, :].rearrange("a n c -> n (a c)"),
                             x1_buf[:, j % 2].rearrange("p q d -> p (q d)")).then_inc(s_x1st[j % 2], 16)
                if exists(k, j + RING):
                    load_x(k, j + RING)
                if 0 <= j < NL:
                    if not (isinstance(k, int) and k == 0):
                        sp.wait_ge(s_wlo, (k - 1) * NL + j + 1)
                    sp.dma_start(w_raw[:, j, :].rearrange("p (a c h) -> p a c h", a=1, c=KC),
                                 w_dram[j][:, bass.ds(k, 1), :, :]).then_inc(s_w[j], 16)

            fill(turn)
            middle(sp, turn)

            def load_x1(t, par):
                sp.dma_start(x1_in[par][:].rearrange("p q d -> p (q d)"),
                             x1_dram[bass.ds(t, 1), :, :].rearrange("a n c -> n (a c)")
                             ).then_inc(s_xb[par], 16)

            sp.wait_ge(s_x1st[0], 16)
            sp.wait_ge(s_bn, 4)
            load_x1(0, 0)
            drain(turn)
            sp.wait_ge(s_x1, NQ)
            sp.wait_ge(s_x1st[1], 16)
            load_x1(1, 1)

            def store(t, par):
                sp.wait_ge(s_out, t + 1)
                sp.dma_start(out[bass.ds(t * Q, Q), :, :].rearrange("b n d -> n b d"),
                             x1_in[par][:]).then_inc(s_outst, 16)

            def tile(t, half, par):
                if not is_first(t):
                    store(t - 1, 1 - par)
                    if not is_last(t):
                        sp.wait_ge(s_outst, t * 16)
                        load_x1(t + 1, 1 - par)

            tiles(sp, tile)
            store(NQ - 1, 1)
            sp.wait_ge(s_outst, 16 * NQ)

        @block.gpsimd
        def _(pool):
            nc.gpsimd.memset(ident[:], 0.0).then_inc(s_ident0, 1)
            nc.gpsimd.memset(ones[:], 1.0).then_inc(s_fill, 1)
            nc.gpsimd.memset(neg_half[:], -0.5).then_inc(s_fill, 1)
            nc.gpsimd.memset(neg_one[:], -1.0).then_inc(s_fill, 1)
            nc.gpsimd.memset(gate_rows[:], 0.0).then_inc(s_fill, 1)
            pool.wait_ge(s_ident0, 1)
            nc.gpsimd.affine_select(out=ident[:], in_=ident[:], compare_op=ALU.not_equal, fill=1.0, base=0,
                                    pattern=[[-1, P]], channel_multiplier=1).then_inc(s_ident, 1)
            nc.gpsimd.memset(acc[:], 0.0).then_inc(s_acc, 1)
            pool.wait_ge(s_fill, 4)

            def rsqrt(which, i, mv, rstd, shift):
                nc.gpsimd.tensor_tensor(neg_mu[:, which], mv[:, :, 0], neg_one[:],
                                        ALU.mult).then_inc(s_step[which], 1)
                nc.gpsimd.tensor_scalar(var_eps[:, which], mv[:, :, 1], LN_EPS, None,
                                        ALU.add).then_inc(s_step[which], 1)
                pool.wait_ge(s_step[which], i * 3 + 2)
                nc.gpsimd.tensor_tensor(rstd, var_eps[:, which], neg_half[:, 0:Q],
                                        ALU.pow).then_inc(s_step[which], 1)
                pool.wait_ge(s_step[which], i * 3 + 3)
                nc.gpsimd.tensor_tensor(shift, neg_mu[:, which], rstd, ALU.mult).then_inc(s_rs[which], 1)

            def turn(k, j):
                s = k * RING + j
                if exists(k, j + 2):
                    slot = (j + 2) % RING
                    pool.wait_ge(s_mv[0], s + 3)
                    if exists(k, j + 1):
                        pool.wait_ge(s_rs[0], s + 2)
                    if exists(k, j - 2):
                        pool.wait_ge(s_h, s - 1)
                    rsqrt(0, s + 2, mv1[:, slot], rstd1[:, slot], shift1[:, slot])
                if exists(k, j - 1):
                    pool.wait_ge(s_mv[1], s)
                    if exists(k, j - 2):
                        pool.wait_ge(s_rs[1], s - 1)
                    cols = bass.ds((s - 1) * Q, Q)
                    rsqrt(1, s - 1, mv2[:, (j - 1) % RING], rstd2[:, cols], shift2[:, cols])
                if exists(k, j - 2) and not is_last_quad(k, j - 2) and not is_last_quad(k, j - 1):
                    pool.wait_ge(s_x2, s - 1)
                    pool.wait_ge(s_acc, s - 1)
                    nc.gpsimd.tensor_tensor(acc[:], acc[:], x2_buf[:, j % 2].rearrange("p q d -> p (q d)"),
                                            ALU.add).then_inc(s_acc, 1)
                if exists(k, j) and 1 <= j <= NL:
                    pool.wait_ge(s_whi, k * NL + j)
                    cols = bass.ds(k * WCOLS, WCOLS)
                    nc.gpsimd.tensor_tensor(w_lo[:, j - 1, cols], w_raw[:, j - 1, :],
                                            w_hi[:, j - 1, cols].bitcast(F32), ALU.subtract).then_inc(s_wlo, 1)

            def bn_rsqrt():
                pool.wait_ge(s_bnvar, 1)
                nc.gpsimd.tensor_tensor(bn_rstd[:].rearrange("p l c -> p (l c)"),
                                        bn_var[:].rearrange("p l c -> p (l c)"), neg_half[:],
                                        ALU.pow).then_inc(s_bnrstd, 1)

            fill(turn, range(-3, 1))
            bn_rsqrt()
            fill(turn, range(1, RING))
            middle(pool, turn)
            drain(turn)

            def residual(t, par):
                pool.wait_ge(s_x2b, t + 1)
                nc.gpsimd.tensor_tensor(x1_in[par][:], x1_in[par][:],
                                        bo_mix[:, None, :].to_broadcast([P, Q, D]), ALU.add).then_inc(s_res, 1)

            pool.wait_ge(s_bo, 1)
            residual(0, 0)

            def tile(t, half, par):
                if not is_last(t):
                    residual(t + 1, 1 - par)

            tiles(pool, tile)

        @block.scalar
        def _(act):
            small = [
                (gate_rows[0:KC, :], gate_weight.rearrange("(c p) o -> c (p o)", p=P)),
                (gate_rows[KC:2 * KC, :], out_gate_weight.rearrange("(c p) o -> c (p o)", p=P)),
                (gate_rows[2 * KC:3 * KC, :], loop_gate.rearrange("(c p) o -> c (p o)", p=P)),
                (gate_rows[NG * KC:NG * KC + 1, :], bias_gate.rearrange("p o -> o p")),
                (gate_rows[NG * KC + 1:NG * KC + 2, :], out_bias_gate.rearrange("p o -> o p")),
                (edge_raw[:, 0, :], edge_bias),
                (edge_raw[:, 1, :], out_edge_bias),
            ]
            assert len(small) == N_CONST
            act.wait_ge(s_fill, 4)
            for dst, src in small:
                act.dma_start(dst, src).then_inc(s_const, 16)

            def x_hi(t, par):
                act.wait_ge(s_xT, t + 1)
                nc.scalar.activation(xh[par][:], xT_ps.rearrange("p c q n -> p (c q n)"),
                                     ACT.Copy).then_inc(s_xh, 1)

            def gate_in(s, j, p):
                act.wait_ge(s_msg, s * 2 + p + 1)
                for q in (2 * p, 2 * p + 1):
                    ins = nc.scalar.activation(t_buf[:, j % 2, q, :], bank[:, 2 + p, (q % 2) * D:(q % 2 + 1) * D],
                                               ACT.Copy, scale=gates[:, j % 2, q, 0:1])
                ins.then_inc(s_t1, 1)

            def weight_hi(k, j):
                act.wait_ge(s_w[j - 1], k * 16 + 16)
                nc.scalar.activation(w_hi[:, j - 1, bass.ds(k * WCOLS, WCOLS)], w_raw[:, j - 1, :],
                                     ACT.Copy).then_inc(s_whi, 1)

            def turn(k, j):
                s = k * RING + j
                if exists(k, j):
                    act.wait_ge(s_gate, s + 1)
                    if exists(k, j - 2):
                        act.wait_ge(s_x1, s - 1)
                    gate_in(s, j, 0)
                if exists(k, j + 1):
                    act.wait_ge(s_hT_ps, s + 2)
                    if exists(k, j):
                        act.wait_ge(s_gate_ps, s + 1)
                    nc.scalar.activation(hT[:].rearrange("p c q n -> p (c q n)"), flat[:, 0:HW],
                                         ACT.Copy).then_inc(s_hT, 1)
                if is_last_quad(k, j):
                    x_hi(0, 0)
                if exists(k, j):
                    gate_in(s, j, 1)
                if exists(k, j + 2):
                    slot = (j + 2) % RING
                    act.wait_ge(s_rs[0], s + 3)
                    if exists(k, j - 2):
                        act.wait_ge(s_x1, s - 1)
                    for q in range(Q):
                        ins = nc.scalar.activation(h_ring[:, slot, q, :], x_ring[:, slot, q, :], ACT.Identity,
                                                   bias=shift1[:, slot, q:q + 1], scale=rstd1[:, slot, q:q + 1])
                    ins.then_inc(s_h, 1)
                elif exists(k, j + 1):
                    norm(0, 0, 0)
                if exists(k, j + 1):
                    act.wait_ge(s_gate_ps, s + 2)
                    if exists(k, j - 1):
                        act.wait_ge(s_x1, s)
                    nc.scalar.activation(gates[:, (j + 1) % 2], gate_ps,
                                         ACT.Sigmoid).then_inc(s_gate, 1)
                if is_last_quad(k, j):
                    weight_hi(k, j)
                    act.wait_ge(s_bn, 4)
                    relu(0, 0, 0)
                if exists(k, j - 1):
                    act.wait_ge(s_rs[1], s)
                    if exists(k, j - 3):
                        act.wait_ge(s_acc, s - 1)
                    for q in range(Q):
                        col = bass.ds((s - 1) * Q + q, 1)
                        ins = nc.scalar.activation(x2_buf[:, (j - 1) % 2, q, :], x1_buf[:, (j - 1) % 2, q, :],
                                                   ACT.Identity, bias=shift2[:, col], scale=rstd2[:, col])
                        if is_last_quad(k, j - 1):
                            ins.then_inc(s_x2last, 1)
                    if not is_last_quad(k, j - 1):
                        ins.then_inc(s_x2, 1)
                if exists(k, j) and 1 <= j <= NL and not is_last_quad(k, j):
                    weight_hi(k, j)

            def norm(t, half, par):
                act.wait_ge(s_xb[par], half * 16 + 16)
                if not is_first(t):
                    act.wait_ge(s_xT, t)
                for q in range(Q):
                    col = bass.ds(t * Q + q, 1)
                    ins = nc.scalar.activation(x2_in[:, q, :], x1_in[par][:, q, :], ACT.Identity,
                                               bias=shift2[:, col], scale=rstd2[:, col])
                ins.then_inc(s_x2b, 1)

            def relu(layer, t, e):
                ready, z, used, done = ((s_l1, z1, s_h1l, s_z1), (s_l2, z2, s_h2l, s_z2))[layer]
                for c in range(KC):
                    act.wait_ge(ready, unit(t, e) * KC + c + 1)
                    if c == 0 and not (is_first(t) and e == 0):
                        act.wait_ge(used, unit(t, e))
                    i = e * KC + c
                    nc.scalar.activation(z[:, c * R:(c + 1) * R], bank[:, 2 * layer + c, :], ACT.Relu,
                                         bias=bn_shift[:, layer, i:i + 1],
                                         scale=bn_scale[:, layer, i:i + 1]).then_inc(done, 1)

            def yT_copy(t):
                act.wait_ge(s_l3, unit(t, E))
                nc.scalar.activation(yT[:].rearrange("p c q n -> p (c q n)"), flat[:, 4 * 512:6 * 512],
                                     ACT.Copy).then_inc(s_yT, 1)

            def softmax_exp():
                act.wait_ge(s_soft, 2)
                nc.scalar.activation(expo[:], bank[:, 4, 0:E], ACT.Exp, bias=neg_max[:],
                                     accum_out=expo_sum[:]).then_inc(s_expo, 1)

            act.wait_ge(s_fill, 4)
            nc.scalar.activation(expo[:, 0:1], ones[:, 0:1], ACT.Sigmoid)
            fill(turn)
            middle(act, turn)
            drain(turn, range(RING))
            nc.scalar.activation(expo[:, 0:1], ones[:, 0:1], ACT.Exp)
            drain(turn, range(RING, RING + 2))
            relu(0, 0, 1)
            softmax_exp()
            relu(1, 0, 0)
            act.wait_ge(s_bc, 2)
            nc.scalar.activation(w_bcast[:, E // 2:].rearrange("p e n -> p (e n)"), bank[:, 5, :],
                                 ACT.Copy).then_inc(s_wb[1], 1)

            def tile(t, half, par):
                for e in range(E):
                    if e == 2 and not is_first(t):
                        yT_copy(t - 1)
                    if e == 5 and not is_last(t):
                        norm(t + 1, half + par, 1 - par)
                    if e == 6 and not is_last(t):
                        if not is_first(t):
                            act.wait_ge(s_l1, unit(t, 0) * KC)
                        x_hi(t + 1, 1 - par)
                    if not (is_first(t) and e < 2):
                        relu(0, t, e)
                    if before(t, e, 1) and not (is_first(t) and e == 1):
                        relu(1, *before(t, e, 1))

            tiles(act, tile)
            relu(1, NQ - 1, E - 1)
            yT_copy(NQ - 1)

        @block.vector
        def _(dve):
            dve.wait_ge(s_adj_in, 16)
            nc.vector.tensor_scalar(adj_min[:], adj_sb[:], 0.0, None, ALU.min).then_inc(s_setup, 1)
            dve.wait_ge(s_setup, 1)
            nc.vector.scalar_tensor_tensor(origin[:], adj_sb[:], 0.0, adj_min[:], ALU.is_gt,
                                           ALU.add).then_inc(s_setup, 1)
            dve.wait_ge(s_setup, 2)
            nc.vector.tensor_tensor(in_mat[:], origin[:], adj_sb[:], ALU.mult).then_inc(s_setup, 1)
            dve.wait_ge(s_adjT, 1)
            nc.vector.tensor_tensor(out_matT[:], bank[:, 7, 0:P], origin[:], ALU.mult).then_inc(s_mats, 1)
            dve.wait_ge(s_inT, 1)
            nc.vector.tensor_copy(in_matT[:], bank[:, 5, 0:P]).then_inc(s_mats, 1)
            dve.wait_ge(s_ident, 1)
            nc.vector.tensor_copy(ident_r[:], ident[:]).then_inc(s_mats, 1)

            def x_lo(t, par):
                dve.wait_ge(s_xh, t + 1)
                nc.vector.tensor_tensor(xl[par][:], xT_ps.rearrange("p c q n -> p (c q n)"),
                                        xh[par][:].bitcast(F32), ALU.subtract).then_inc(s_xl, 1)

            def stats(which, src, i):
                for q in range(Q):
                    ins = nc.vector.bn_stats(bn6[:, which, q, :], src[:, q, :])
                ins.then_inc(s_bn6[which], 1)

            def mean_var(which, dst):
                for q in range(Q):
                    ins = nc.vector.bn_aggr(dst[:, q, :], bn6[:, which, q, :])
                ins.then_inc(s_mv[which], 1)

            def turn(k, j):
                s = k * RING + j
                here, ahead = exists(k, j), exists(k, j + 3)
                slot = (j + 3) % RING
                if exists(k, j - 1):
                    dve.wait_ge(s_bn6[1], s)
                    if exists(k, j - RING):
                        dve.wait_ge(s_rs[1], s - RING + 1)
                if here:
                    for p in range(2):
                        if is_last_quad(k, j) and p == 1:
                            x_lo(0, 0)
                        dve.wait_ge(s_t1, s * 2 + p + 1)
                        for q in (2 * p, 2 * p + 1):
                            t = t_buf[:, j % 2, q, :]
                            ins = nc.vector.scalar_tensor_tensor(
                                t, bank[:, 4 + p, (q % 2) * D:(q % 2 + 1) * D], gates[:, j % 2, q, 1:2], t,
                                ALU.mult, ALU.add)
                        ins.then_inc(s_t2, 1)
                if exists(k, j - 1):
                    mean_var(1, mv2[:, (j - 1) % RING])
                if here:
                    for p in range(2):
                        dve.wait_ge(s_t2, s * 2 + p + 1)
                        for q in (2 * p, 2 * p + 1):
                            t = t_buf[:, j % 2, q, :]
                            ins = nc.vector.scalar_tensor_tensor(t, h_ring[:, j % RING, q, :],
                                                                 gates[:, j % 2, q, 2:3], t, ALU.mult, ALU.add)
                    ins.then_inc(s_t3, 1)
                if ahead:
                    dve.wait_ge(s_x[slot], (k + (j + 3) // RING) * 16 + 16)
                    if exists(k, j + 2):
                        dve.wait_ge(s_mv[0], s + 3)
                    stats(0, x_ring[:, slot], s + 3)
                if ahead:
                    dve.wait_ge(s_bn6[0], s + 4)
                    if exists(k, j - 1):
                        dve.wait_ge(s_rs[0], s)
                if here:
                    dve.wait_ge(s_t3, s + 1)
                    if exists(k, j - 2):
                        dve.wait_ge(s_x1st[j % 2], (k * 2 + j // 2) * 16)
                        dve.wait_ge(s_x2, s - 1)
                    nc.vector.scalar_tensor_tensor(
                        x1_buf[:, j % 2].rearrange("p q d -> p (q d)"),
                        t_buf[:, j % 2].rearrange("p q d -> p (q d)"), 0.0,
                        x_ring[:, j % RING].rearrange("p q d -> p (q d)"), ALU.max, ALU.add).then_inc(s_x1, 1)
                if ahead:
                    mean_var(0, mv1[:, slot])
                if here:
                    dve.wait_ge(s_x1, s + 1)
                    if exists(k, j - 1):
                        dve.wait_ge(s_mv[1], s)
                    stats(1, x1_buf[:, j % 2], s)

            fill(turn, range(-3, -1))
            dve.wait_ge(s_const, 16 * N_CONST)
            nc.vector.tensor_copy(edge_hi[:], edge_raw[:]).then_inc(s_mats, 1)
            dve.wait_ge(s_gateT, 1)
            nc.vector.tensor_copy(gate_cols[:], bank[:, 6, 0:GR]).then_inc(s_mats, 1)
            dve.wait_ge(s_mats, 5)
            nc.vector.tensor_tensor(edge_lo[:], edge_raw[:], edge_hi[:].bitcast(F32),
                                    ALU.subtract).then_inc(s_mats, 1)
            fill(turn, range(-1, 0))
            G_, BE, M_, V_, B_ = range(5)
            dve.wait_ge(s_bnT, 1)
            nc.vector.tensor_copy(bn_cols[:].rearrange("p l i c -> p (l i c)"),
                                  bank[:, 7, 0:10 * EC]).then_inc(s_setup, 1)
            dve.wait_ge(s_setup, 4)
            nc.vector.tensor_scalar(bn_var[:], bn_cols[:, :, V_, :], BN_EPS, None, ALU.add).then_inc(s_bnvar, 1)
            nc.vector.tensor_tensor(bn_diff[:], bn_cols[:, :, B_, :], bn_cols[:, :, M_, :],
                                    ALU.subtract).then_inc(s_bn, 1)
            fill(turn, range(1))
            dve.wait_ge(s_bnrstd, 1)
            nc.vector.tensor_tensor(bn_scale[:], bn_cols[:, :, G_, :], bn_rstd[:], ALU.mult).then_inc(s_bn, 1)
            dve.wait_ge(s_bn, 2)
            nc.vector.tensor_tensor(bn_prod[:], bn_diff[:], bn_scale[:], ALU.mult).then_inc(s_bn, 1)
            dve.wait_ge(s_bn, 3)
            nc.vector.tensor_tensor(bn_shift[:], bn_prod[:], bn_cols[:, :, BE, :], ALU.add).then_inc(s_bn, 1)
            fill(turn, range(1, RING))
            middle(dve, turn)

            def split1(t, e):
                i = unit(t, e)
                dve.wait_ge(s_z1, i * KC + KC)
                if before(t, e, 2):
                    dve.wait_ge(s_l2, (i - 1) * KC)
                nc.vector.tensor_copy(h1h[:, e % 2], z1[:]).then_inc(s_h1h, 1)
                dve.wait_ge(s_h1h, i + 1)
                nc.vector.tensor_tensor(h1l[:, e % 2], z1[:], h1h[:, e % 2].bitcast(F32),
                                        ALU.subtract).then_inc(s_h1l, 1)

            def split2(t, e):
                i = unit(t, e)
                dve.wait_ge(s_z2, i * KC + KC)
                z = z2[:].rearrange("p (a n) -> p a n", n=N)
                nc.vector.tensor_tensor(z, z, w_bcast[:, e:e + 1, :].to_broadcast([P, KC * Q, N]),
                                        ALU.mult).then_inc(s_z2w, 1)
                dve.wait_ge(s_z2w, i + 1)
                if before(t, e, 1):
                    dve.wait_ge(s_l3, i)
                nc.vector.tensor_copy(h2h[:], z2[:]).then_inc(s_h2h, 1)
                dve.wait_ge(s_h2h, i + 1)
                nc.vector.tensor_tensor(h2l[:], z2[:], h2h[:].bitcast(F32), ALU.subtract).then_inc(s_h2l, 1)

            def output(t, par):
                dve.wait_ge(s_y, t + 1)
                dve.wait_ge(s_res, t + 1)
                nc.vector.tensor_tensor(x1_in[par][:], y_ps, x1_in[par][:], ALU.add).then_inc(s_out, 1)

            drain(turn)
            split1(0, 0)

            dve.wait_ge(s_x2, NQ - 1)
            dve.wait_ge(s_acc, NQ - 1)
            nc.vector.tensor_tensor(acc[:], acc[:], x2_buf[:, (NQ - 2) % 2].rearrange("p q d -> p (q d)"),
                                    ALU.add).then_inc(s_acc, 1)
            dve.wait_ge(s_acc, NQ)
            nc.vector.tensor_tensor(acc[:, 0:2 * D], acc[:, 0:2 * D], acc[:, 2 * D:4 * D],
                                    ALU.add).then_inc(s_fold, 1)
            dve.wait_ge(s_fold, 1)
            nc.vector.tensor_tensor(acc[:, 0:D], acc[:, 0:D], acc[:, D:2 * D], ALU.add).then_inc(s_fold, 1)

            dve.wait_ge(s_featT, 1)
            nc.vector.tensor_scalar(featT[:], bank[:, 5, 0:D], 1.0 / B, None, ALU.mult).then_inc(s_soft, 1)
            dve.wait_ge(s_logit, 1)
            nc.vector.tensor_reduce(neg_max[:], bank[:, 4, 0:E], AX_X, ALU.max, negate=True).then_inc(s_soft, 1)
            dve.wait_ge(s_expo, 1)
            nc.vector.reciprocal(expo_inv[:], expo_sum[:]).then_inc(s_soft, 1)
            dve.wait_ge(s_soft, 3)
            nc.vector.tensor_scalar(w_soft[:], expo[:], expo_inv[:], None, ALU.mult).then_inc(s_soft, 1)
            dve.wait_ge(s_soft, 4)
            nc.vector.tensor_tensor(w_diag[:], ident[:, None, :].to_broadcast([P, E, N]),
                                    w_soft[:, :, None].to_broadcast([P, E, N]), ALU.mult).then_inc(s_soft, 1)
            split1(0, 1)
            dve.wait_ge(s_x1st[0], 16 * (NQ // 2))
            dve.wait_ge(s_x1st[1], 16 * (NQ // 2))
            dve.wait_ge(s_bc, 1)
            nc.vector.tensor_copy(w_bcast[:, 0:E // 2].rearrange("p e n -> p (e n)"),
                                  bank[:, 4, :]).then_inc(s_wb[0], 1)
            dve.wait_ge(s_wb[0], 1)
            split2(0, 0)
            dve.wait_ge(s_wb[1], 1)
            dve.wait_ge(s_wT, 1)
            nc.vector.tensor_copy(wT[:], bank[0:E, 6, 0:P]).then_inc(s_soft, 1)

            def tile(t, half, par):
                for e in range(E):
                    if e == 3 and not is_first(t):
                        output(t - 1, 1 - par)
                    if e == 6 and not is_last(t):
                        x_lo(t + 1, 1 - par)
                    if not (is_first(t) and e < 2):
                        split1(t, e)
                    if before(t, e, 1) and not (is_first(t) and e == 1):
                        split2(*before(t, e, 1))
                    if is_first(t) and e == 3:
                        dve.wait_ge(s_mix, 1)
                        nc.vector.tensor_copy(bo_mix[:], bank[:, 7, 0:D]).then_inc(s_bo, 1)

            tiles(dve, tile)
            split2(NQ - 1, E - 1)
            output(NQ - 1, 1)

        @block.tensor
        def _(pe):
            pe.wait_ge(s_adj_in, 16)
            pe.wait_ge(s_ident, 1)
            nc.tensor.transpose(bank[:, 7, 0:P], adj_sb[:], ident[:]).then_inc(s_adjT, 1)
            pe.wait_ge(s_setup, 3)
            nc.tensor.transpose(bank[:, 5, 0:P], in_mat[:], ident[:]).then_inc(s_inT, 1)
            for _ in range(N_WARM):
                nc.tensor.matmul(bank[:, 0, 0:P], ident[:], ident[:], start=True, stop=True)
            pe.wait_ge(s_const, 16 * N_CONST)
            nc.tensor.transpose(bank[:, 6, 0:GR], gate_rows[:], ident[0:GR, 0:GR]).then_inc(s_gateT, 1)

            def bn_transposes():
                pe.wait_ge(s_late, 16 * N_LATE)
                for layer in range(2):
                    for i in range(5):
                        o = (layer * 5 + i) * EC
                        ins = nc.tensor.transpose(bank[:, 7, o:o + EC], bn_rows[:, layer, i, :],
                                                  ident[0:EC, 0:EC])
                ins.then_inc(s_bnT, 1)

            def x_transposes(t):
                pe.wait_ge(s_x2b, t + 1)
                for c in range(KC):
                    for q in range(Q):
                        ins = nc.tensor.transpose(xT_ps[:, c, q, :], x2_in[:, q, c * P:(c + 1) * P], ident[:])
                ins.then_inc(s_xT, 1)

            def messages(s, k, j, p):
                if p == 0:
                    pe.wait_ge(s_h, s + 1)
                if exists(k, j - 1):
                    pe.wait_ge(s_t1, s * 2 + p - 1)
                    pe.wait_ge(s_t2, s * 2 + p - 1)
                moving = h_ring[:, j % RING, 2 * p:2 * p + 2, :]
                for i, matT in enumerate((in_matT, out_matT)):
                    dst = bank[:, 2 + 2 * i + p, :].rearrange("p (q d) -> p q d", q=2)
                    nc.tensor.matmul(dst, matT[:], moving, start=True, stop=False)
                    nc.tensor.matmul(dst, ident_r[:], edge_hi[:, i:i + 1, :].to_broadcast([P, 2, D]),
                                     start=False, stop=False)
                    ins = nc.tensor.matmul(dst, ident_r[:], edge_lo[:, i:i + 1, :].to_broadcast([P, 2, D]),
                                           start=False, stop=True)
                ins.then_inc(s_msg, 1)

            def turn(k, j):
                s = k * RING + j
                if exists(k, j):
                    messages(s, k, j, 0)
                if exists(k, j + 1):
                    pe.wait_ge(s_h, s + 2)
                    if exists(k, j):
                        pe.wait_ge(s_hT, s + 1)
                    for q in range(Q):
                        for c in range(KC):
                            ins = nc.tensor.transpose(hT_ps[:, c, q, :],
                                                      h_ring[:, (j + 1) % RING, q, c * P:(c + 1) * P], ident[:])
                    ins.then_inc(s_hT_ps, 1)
                if is_last_quad(k, j):
                    pe.wait_ge(s_gate, NQ)
                    x_transposes(0)
                if exists(k, j):
                    messages(s, k, j, 1)
                if exists(k, j + 1):
                    pe.wait_ge(s_hT, s + 2)
                    if isinstance(k, int) and s == -1:
                        pe.wait_ge(s_mats, 6)
                    if exists(k, j):
                        pe.wait_ge(s_gate, s + 1)
                    nc.tensor.matmul(gate_ps, ident[:], gate_cols[:, None, NG * KC:].to_broadcast([P, Q, NG]),
                                     start=True, stop=False, skip_group_check=True)
                    for q in range(Q):
                        for c in range(KC):
                            ins = nc.tensor.matmul(gate_ps[:, q, :], hT[:, c, q, :], gate_cols[:, c:NG * KC:KC],
                                                   start=False, stop=(q == Q - 1 and c == KC - 1),
                                                   skip_group_check=True)
                    ins.then_inc(s_gate_ps, 1)

            def y_transposes(t):
                pe.wait_ge(s_yT, t + 1)
                for q in range(Q):
                    for c in range(KC):
                        ins = nc.tensor.transpose(y_ps[:, q, c * P:(c + 1) * P], yT[:, c, q, :], ident[:])
                ins.then_inc(s_y, 1)

            def layer(n, e, h, dst, hi, lo, lo_sem, lo_count, first=True, last=True):
                for c in range(KC):
                    rows = slice(c * R, (c + 1) * R)
                    nc.tensor.matmul(dst, w_at(w_hi, n, e, c, h), hi[:, rows], start=(first and c == 0),
                                     stop=False)
                    nc.tensor.matmul(dst, w_at(w_lo, n, e, c, h), hi[:, rows], start=False, stop=False)
                if h == 0:
                    pe.wait_ge(lo_sem, lo_count)
                for c in range(KC):
                    rows = slice(c * R, (c + 1) * R)
                    ins = nc.tensor.matmul(dst, w_at(w_hi, n, e, c, h), lo[:, rows], start=False,
                                           stop=(last and c == KC - 1))
                return ins

            def layer1(t, par, e):
                if e == 0:
                    pe.wait_ge(s_xh, t + 1)
                for h in range(KC):
                    if before(t, e, 1):
                        pe.wait_ge(s_z1, unit(t, e - 1) * KC + h + 1)
                    layer(0, e, h, bank[:, h, :], xh[par][:], xl[par][:],
                          s_xl, t + 1).then_inc(s_l1, 1)

            def layer2(t, e):
                i = unit(t, e)
                pe.wait_ge(s_h1h, i + 1)
                for h in range(KC):
                    if before(t, e, 1):
                        pe.wait_ge(s_z2, (i - 1) * KC + h + 1)
                    layer(1, e, h, bank[:, 2 + h, :], h1h[:, e % 2], h1l[:, e % 2],
                          s_h1l, i + 1).then_inc(s_l2, 1)

            def layer3(t, e):
                pe.wait_ge(s_h2h, unit(t, e) + 1)
                if e == 0 and not is_first(t):
                    pe.wait_ge(s_yT, t)
                for h in range(KC):
                    ins = layer(2, e, h, bank[:, 4 + h, :], h2h, h2l, s_h2l, unit(t, e) + 1,
                                first=(e == 0), last=(e == E - 1))
                ins.then_inc(s_l3, 1)

            pe.wait_ge(s_fill, 4)
            fill(turn, range(-3, 0))
            bn_transposes()
            fill(turn, range(RING))
            middle(pe, turn)
            drain(turn, range(RING))

            def logits():
                pe.wait_ge(s_t2, 2 * NQ)
                pe.wait_ge(s_fold, 2)
                for c in range(KC):
                    nc.tensor.matmul(bank[:, 5, c * P:(c + 1) * P], acc[:, c * P:(c + 1) * P], ident[:],
                                     start=(c == 0), stop=False, skip_group_check=True)
                for q in range(Q):
                    pe.wait_ge(s_x2last, q + 1)
                    for c in range(KC):
                        ins = nc.tensor.matmul(bank[:, 5, c * P:(c + 1) * P],
                                               x2_buf[:, (NQ - 1) % 2, q, c * P:(c + 1) * P], ident[:],
                                               start=False, stop=(q == Q - 1 and c == KC - 1),
                                               skip_group_check=True)
                ins.then_inc(s_featT, 1)
                pe.wait_ge(s_soft, 1)
                dst = bank[:, 4, 0:E]
                nc.tensor.matmul(dst, ones[0:1, :], br_sb[:], start=True, stop=False)
                for c in range(KC):
                    ins = nc.tensor.matmul(dst, featT[:, c * P:(c + 1) * P], wr_sb[:, c, :], start=False,
                                           stop=(c == KC - 1))
                ins.then_inc(s_logit, 1)

            def spread_w():
                pe.wait_ge(s_soft, 5)
                for i in range(2):
                    nc.tensor.matmul(bank[:, 4 + i, :], ones[:],
                                     w_diag[:, 4 * i:4 * i + 4, :].rearrange("p e n -> p (e n)"),
                                     start=True, stop=True).then_inc(s_bc, 1)
                nc.tensor.transpose(bank[0:E, 6, 0:P], w_soft[:], ident[:]).then_inc(s_wT, 1)

            def mix_bo():
                pe.wait_ge(s_soft, 6)
                nc.tensor.matmul(bank[:, 7, 0:D], wT[:], bo_sb[:], start=True, stop=True).then_inc(s_mix, 1)

            def tile(t, half, par):
                for e in range(E):
                    if e == 3 and not is_first(t):
                        y_transposes(t - 1)
                    if e == 6 and not is_last(t):
                        if not is_first(t):
                            pe.wait_ge(s_out, t)
                        else:
                            pe.wait_ge(s_xl, 1)
                            pe.wait_ge(s_bo, 1)
                        x_transposes(t + 1)
                    if is_first(t) and e == 2:
                        logits()
                    if is_first(t) and e == 3:
                        mix_bo()
                    layer1(t, par, e)
                    if is_first(t) and e == 2:
                        spread_w()
                    if before(t, e, 1):
                        layer2(*before(t, e, 1))
                    if is_first(t) and e == 2:
                        pe.wait_ge(s_wb[0], 1)
                        pe.wait_ge(s_wb[1], 1)
                    if before(t, e, 2):
                        layer3(*before(t, e, 2))

            tiles(pe, tile)
            layer2(NQ - 1, E - 1)
            layer3(NQ - 1, E - 2)
            layer3(NQ - 1, E - 1)
            y_transposes(NQ - 1)


_INS = ['x', 'adj', 'L0_gnn_edge_bias', 'L0_gnn_gate_weight', 'L0_gnn_bias_gate', 'L0_gnn_out_edge_bias',
        'L0_gnn_out_gate_weight', 'L0_gnn_out_bias_gate', 'L0_gnn_loop_gate', 'L0_ffn_Wr', 'L0_ffn_br', 'L0_ffn_W1',
        'L0_ffn_b1', 'L0_ffn_g1', 'L0_ffn_be1', 'L0_ffn_m1', 'L0_ffn_v1', 'L0_ffn_W2', 'L0_ffn_b2', 'L0_ffn_g2',
        'L0_ffn_be2', 'L0_ffn_m2', 'L0_ffn_v2', 'L0_ffn_Wo', 'L0_ffn_bo']
_OUTS = [((128, 128, 256), 'float32')]


def kernel(**inputs):
    import numpy as _np
    import concourse.bacc as _bacc
    from concourse import mybir as _mybir
    from concourse.bass_utils import run_bass_kernel_spmd as _run

    nc = _bacc.Bacc("TRN2", target_bir_lowering=False, num_devices=1)
    arrays, args = {}, []
    for name in _INS:
        a = _np.ascontiguousarray(inputs[name])
        arrays[f"in_{name}_dram"] = a
        args.append(nc.dram_tensor(f"in_{name}_dram", a.shape, _mybir.dt.from_np(a.dtype), kind="ExternalInput").ap())
    for i, (shape, dtype) in enumerate(_OUTS):
        dt = _mybir.dt.from_np(_np.dtype(dtype))
        args.append(nc.dram_tensor(f"out_{i}_dram", shape, dt, kind="ExternalOutput").ap())
    adj_ffn_kernel(nc, *args)
    r = _run(nc, [arrays], core_ids=[0])
    got = tuple(r.results[0][f"out_{i}_dram"] for i in range(len(_OUTS)))
    return got[0]
```
